# Optimizing a Trainium2 kernel written in Bass

```python
import numpy as np
import jax
import jax.numpy as jnp

def _softmax(x, axis=-1):
    return jax.nn.softmax(x, axis=axis)
def _gelu(x):
    return jax.nn.gelu(x, approximate=True)
def _silu(x):
    return jax.nn.silu(x)
def _sigmoid(x):
    return jax.nn.sigmoid(x)
def _layernorm(x, axis=-1, eps=1e-5):
    m = jnp.mean(x, axis=axis, keepdims=True)
    v = jnp.var(x, axis=axis, keepdims=True)
    return (x - m) / jnp.sqrt(v + eps)
def _scatter_add(tgt, idx, src, axis=0):
    return tgt.at[idx].add(src)
def _segment_sum(src, seg, n):
    return jax.ops.segment_sum(src, seg, n)

kernel_name = 'mk_early_fusion_d1_tok_img256_08f12c'

def setup_inputs(seed: int = 0):
    np.random.seed(seed)
    _w = jnp.asarray
    def _rec_inputs():
        import jax
        import jax.numpy as jnp
        _rk = jax.random.key(seed)
        x = (-0.000395706 + 0.999959 * jax.random.normal(jax.random.fold_in(_rk, 1), (8, 1, 224, 224), jnp.float32))
        txt = (0.50093 + 0.651177 * jax.random.normal(jax.random.fold_in(_rk, 2), (8, 77, 256), jnp.float32))
        return x, txt
    x, txt = _rec_inputs()
    def _L0_tok_setup():
        import jax, jax.numpy as jnp
        import numpy as np
        IMAGE_SIZE = 224
        PATCH_SIZE = 7
        EMBED_DIM = 256
        NUM_PATCHES = (IMAGE_SIZE // PATCH_SIZE) ** 2
        PATCH_DIM = PATCH_SIZE ** 2
        key = jax.random.key(seed)
        kx, kw, kb, kp = jax.random.split(key, 4)
        x = jax.random.normal(kx, (256, 1, IMAGE_SIZE, IMAGE_SIZE), dtype=jnp.float32)
        bound = 1.0 / np.sqrt(PATCH_DIM)
        W = jax.random.uniform(kw, (EMBED_DIM, PATCH_DIM), minval=-bound, maxval=bound, dtype=jnp.float32)
        b = jax.random.uniform(kb, (EMBED_DIM,), minval=-bound, maxval=bound, dtype=jnp.float32)
        pos = jax.random.uniform(kp, (1, NUM_PATCHES, EMBED_DIM), dtype=jnp.float32)
        return {'x': x, 'W': W, 'b': b, 'pos': pos}
    _L0_tok_all = _L0_tok_setup()
    _L0_tok_in = {k: v for k, v in _L0_tok_all.items() if k in ('W', 'b', 'pos', )}
    del _L0_tok_all

    def _L0_attn_setup():
        import jax, jax.numpy as jnp
        import numpy as np
        import math
        B, S, D = (4, 4096, 256)
        key = jax.random.key(seed)
        ks = jax.random.split(key, 9)
        s = 1.0 / math.sqrt(D)
        return {'src': jax.random.normal(ks[0], (B, S, D), dtype=jnp.float32), 'Wq': jax.random.normal(ks[1], (D, D), dtype=jnp.float32) * s, 'bq': jax.random.normal(ks[2], (D,), dtype=jnp.float32) * s, 'Wk': jax.random.normal(ks[3], (D, D), dtype=jnp.float32) * s, 'bk': jax.random.normal(ks[4], (D,), dtype=jnp.float32) * s, 'Wv': jax.random.normal(ks[5], (D, D), dtype=jnp.float32) * s, 'bv': jax.random.normal(ks[6], (D,), dtype=jnp.float32) * s, 'Wo': jax.random.normal(ks[7], (D, D), dtype=jnp.float32) * s, 'bo': jax.random.normal(ks[8], (D,), dtype=jnp.float32) * s}
    _L0_attn_all = _L0_attn_setup()
    _L0_attn_in = {k: v for k, v in _L0_attn_all.items() if k in ('Wq', 'bq', 'Wk', 'bk', 'Wv', 'bv', 'Wo', 'bo', )}
    del _L0_attn_all

    def _L0_ffn_setup():
        import math
        import jax, jax.numpy as jnp
        import numpy as np
        CAPACITY_FACTOR = 1.25
        TOP_K = 2
        LN_EPS = 1e-05

        def _layer_norm(x, gamma, beta):
            mu = jnp.mean(x, axis=-1, keepdims=True)
            var = jnp.var(x, axis=-1, keepdims=True)
            return (x - mu) * jax.lax.rsqrt(var + LN_EPS) * gamma + beta
        key = jax.random.key(seed)
        ks = jax.random.split(key, 4)
        B, S, D, F, E = (8, 4096, 256, 512, 8)
        x = jax.random.normal(ks[0], (B, S, D), dtype=jnp.float32)
        Wr = jax.random.normal(ks[1], (D, E), dtype=jnp.float32) / np.sqrt(D)
        br = jnp.zeros((E,), jnp.float32)
        W1 = jax.random.normal(ks[2], (E, D, F), dtype=jnp.float32) / np.sqrt(D)
        b1 = jnp.zeros((E, F), jnp.float32)
        W2 = jax.random.normal(ks[3], (E, F, D), dtype=jnp.float32) / np.sqrt(F)
        b2 = jnp.zeros((E, D), jnp.float32)
        gamma = jnp.ones((D,), jnp.float32)
        beta = jnp.zeros((D,), jnp.float32)
        return {'x': x, 'Wr': Wr, 'br': br, 'W1': W1, 'b1': b1, 'W2': W2, 'b2': b2, 'gamma': gamma, 'beta': beta}
    _L0_ffn_all = _L0_ffn_setup()
    _L0_ffn_in = {k: v for k, v in _L0_ffn_all.items() if k in ('Wr', 'br', 'W1', 'b1', 'W2', 'b2', 'gamma', 'beta', )}
    del _L0_ffn_all

    return {
        "x": x,
        "txt": txt,
        "L0_tok_W": _L0_tok_in["W"],
        "L0_tok_b": _L0_tok_in["b"],
        "L0_tok_pos": _L0_tok_in["pos"],
        "L0_attn_Wq": _L0_attn_in["Wq"],
        "L0_attn_bq": _L0_attn_in["bq"],
        "L0_attn_Wk": _L0_attn_in["Wk"],
        "L0_attn_bk": _L0_attn_in["bk"],
        "L0_attn_Wv": _L0_attn_in["Wv"],
        "L0_attn_bv": _L0_attn_in["bv"],
        "L0_attn_Wo": _L0_attn_in["Wo"],
        "L0_attn_bo": _L0_attn_in["bo"],
        "L0_ffn_Wr": _L0_ffn_in["Wr"],
        "L0_ffn_br": _L0_ffn_in["br"],
        "L0_ffn_W1": _L0_ffn_in["W1"],
        "L0_ffn_b1": _L0_ffn_in["b1"],
        "L0_ffn_W2": _L0_ffn_in["W2"],
        "L0_ffn_b2": _L0_ffn_in["b2"],
        "L0_ffn_gamma": _L0_ffn_in["gamma"],
        "L0_ffn_beta": _L0_ffn_in["beta"],
    }

def reference(x, txt, L0_tok_W, L0_tok_b, L0_tok_pos, L0_attn_Wq, L0_attn_bq, L0_attn_Wk, L0_attn_bk, L0_attn_Wv, L0_attn_bv, L0_attn_Wo, L0_attn_bo, L0_ffn_Wr, L0_ffn_br, L0_ffn_W1, L0_ffn_b1, L0_ffn_W2, L0_ffn_b2, L0_ffn_gamma, L0_ffn_beta):
    import jax
    import jax.numpy as jnp
    def _L0_tok_ref(x, W, b, pos):
        import jax, jax.numpy as jnp
        import numpy as np
        IMAGE_SIZE = 224
        PATCH_SIZE = 7
        EMBED_DIM = 256
        NUM_PATCHES = (IMAGE_SIZE // PATCH_SIZE) ** 2
        PATCH_DIM = PATCH_SIZE ** 2
        B = x.shape[0]
        p = PATCH_SIZE
        n = IMAGE_SIZE // p
        patches = x.reshape(B, n, p, n, p).transpose(0, 1, 3, 2, 4).reshape(B, n * n, p * p)
        out = jnp.einsum('bnd,ed->bne', patches, W) + b + pos
        return out

    def _L0_attn_ref(src, Wq, bq, Wk, bk, Wv, bv, Wo, bo):
        import jax, jax.numpy as jnp
        import numpy as np
        import math
        B, S, D = (4, 4096, 256)
        q = src @ Wq.T + bq
        k = src @ Wk.T + bk
        v = src @ Wv.T + bv
        row_mask = (q[:, :, 0] != 0) & (k[:, :, 0] != 0)
        mask = row_mask[:, :, None]
        scale = 1.0 / math.sqrt(D)
        scores = jnp.einsum('bid,bjd->bij', q, k) * scale
        scores = jnp.where(mask, scores, jnp.float32(-1000000000.0))
        prob = jax.nn.softmax(scores, axis=-1)
        prob = jnp.where(mask, prob, 0.0)
        out = jnp.einsum('bij,bjd->bid', prob, v)
        return out @ Wo.T + bo

    def _L0_ffn_ref(x, Wr, br, W1, b1, W2, b2, gamma, beta):
        import math
        import jax, jax.numpy as jnp
        import numpy as np
        CAPACITY_FACTOR = 1.25
        TOP_K = 2
        LN_EPS = 1e-05

        def _layer_norm(x, gamma, beta):
            mu = jnp.mean(x, axis=-1, keepdims=True)
            var = jnp.var(x, axis=-1, keepdims=True)
            return (x - mu) * jax.lax.rsqrt(var + LN_EPS) * gamma + beta
        B, S, D = x.shape
        E = Wr.shape[1]
        N = B * S
        K = TOP_K
        logits = jnp.mean(x, axis=1) @ Wr + br
        routing_weights = jax.nn.softmax(logits, axis=-1)
        capacity = float(math.ceil(N * CAPACITY_FACTOR / E))
        expected_loads = routing_weights.sum(axis=0) * (N / B)
        scale = jnp.where(expected_loads > capacity, capacity / expected_loads, 1.0)
        routing_weights = jax.nn.softmax(routing_weights * scale, axis=-1)
        rw_tok = jnp.broadcast_to(routing_weights[:, None, :], (B, S, E)).reshape(N, E)
        top_w, top_i = jax.lax.top_k(rw_tok, K)
        top_w = jax.nn.softmax(top_w, axis=-1)
        xf = x.reshape(N, D)
        h = jax.nn.gelu(jnp.einsum('nd,edf->enf', xf, W1) + b1[:, None, :], approximate=False)
        y = jnp.einsum('enf,efd->end', h, W2) + b2[:, None, :]
        w_dense = jnp.zeros((N, E), x.dtype).at[jnp.arange(N)[:, None], top_i].add(top_w)
        out = jnp.einsum('ne,end->nd', w_dense, y).reshape(B, S, D)
        out = _layer_norm(out + x, gamma, beta)
        return out

    h = _L0_tok_ref(x, L0_tok_W, L0_tok_b, L0_tok_pos)
    h = jnp.concatenate([h, txt], axis=1)
    h = h + _L0_attn_ref(_layernorm(h, axis=-1), L0_attn_Wq, L0_attn_bq, L0_attn_Wk, L0_attn_bk, L0_attn_Wv, L0_attn_bv, L0_attn_Wo, L0_attn_bo)
    h = h + _L0_ffn_ref(_layernorm(h, axis=-1), L0_ffn_Wr, L0_ffn_br, L0_ffn_W1, L0_ffn_b1, L0_ffn_W2, L0_ffn_b2, L0_ffn_gamma, L0_ffn_beta)
    return h


_drawn_inputs = setup_inputs


def setup_inputs(seed=0):
    import zlib

    import numpy as np

    out = dict(_drawn_inputs(seed))
    spreads = {'L0_ffn_br': (0.0, 0.1),
     'L0_ffn_b1': (0.0, 0.311),
     'L0_ffn_b2': (0.0, 0.1),
     'L0_ffn_gamma': (1.0, 0.2),
     'L0_ffn_beta': (0.0, 0.1)}
    factors = {'L0_attn_bq': 5.196, 'L0_attn_bk': 8.0}
    for name, (base, spread) in spreads.items():
        noise = np.random.default_rng([zlib.crc32(name.encode()), seed]).standard_normal(out[name].shape)
        drawn = base * np.exp(spread * noise) if base else spread * noise
        out[name] = jnp.asarray(drawn.astype(out[name].dtype))
    for name, factor in factors.items():
        out[name] = (out[name] * factor).astype(out[name].dtype)
    return out
```

```python
from contextlib import ExitStack

import concourse.bass as bass
from concourse import mybir

F32 = mybir.dt.float32
F32R = mybir.dt.float32r
U32 = mybir.dt.uint32
I32 = mybir.dt.int32
ALU = mybir.AluOpType
ACT = mybir.ActivationFunctionType
AX_X = mybir.AxisListType.X
AX_XY = mybir.AxisListType.XY

P = 128
NB = 8
IMG, PATCH = 224, 7
SIDE = IMG // PATCH
NIMG = SIDE * SIDE
PD = PATCH * PATCH
NTXT = 77
S = NIMG + NTXT
D = 256
DH = D // P
NE, F = 8, 512
FQ = F // P
TOPK = 2
NT = (S + P - 1) // P
TC = 3
NC = NT // TC
CW = TC * P
LASTR = S - (NT - 1) * P
LASTW = S - (NC - 1) * CW
SW = S // 3
SE = S + S % 2
VW = D + 4
EPS = 1e-5
SCALE = 1.0 / float(D) ** 0.5
assert SW * 3 == S and SW % 2 and 3 * SW + 1 <= SE
CAPACITY = float(-(-(NB * S * 5 // 4 + (1 if NB * S * 5 % 4 else 0)) // NE))
NIT = NIMG // P
NF = TOPK * FQ
NPG = 2 * SIDE // 4
GPI = SIDE // 4


def build(nc, x, txt, Wt, bt, pos, Wq, bq, Wk, bk, Wv, bv, Wo, bo, Wr, br, W1, b1, W2, b2, gamma, beta, out):
    with ExitStack() as ctx:
        def sb(name, shape, dt=F32, into=ctx):
            return into.enter_context(nc.sbuf_tensor(name, shape, dt))

        def sem(name):
            return ctx.enter_context(nc.semaphore(name))

        Z = sb("Z", [P, NB * NT, D])
        ident = sb("ident", [P, P])
        ones = sb("ones", [P, P])
        half_neg = sb("half_neg", [P, TC])
        rstd2 = sb("rstd2", [P, NB * NT])
        nmr2 = sb("nmr2", [P, NB * NT])
        bo_row = sb("bo_row", [P, D])
        acc = sb("acc", [P, NB, D])
        wr_sb = sb("wr_sb", [P, DH, NE])
        br_row = sb("br_row", [NB, NE])
        route_w = sb("route_w", [P, NB * TOPK])
        route_i = sb("route_i", [1, NB * TOPK], I32)

        ph = ExitStack()
        xT_hi = sb("xT_hi", [P, 2, DH, SE], F32R, ph)
        xT_lo = sb("xT_lo", [P, 2, DH, SE], F32R, ph)
        xs_hi = sb("xs_hi", [P, DH, CW], F32R, ph)
        xs_lo = sb("xs_lo", [P, DH, CW], F32R, ph)
        wl = ExitStack()
        img = sb("img", [P, 2, PATCH * IMG], F32, wl)
        imp = sb("imp", [P, 2, SIDE, PD], F32, wl)
        wq_sb = sb("wq_sb", [P, DH, D], F32, wl)
        wk_sb = sb("wk_sb", [P, DH, D], F32, wl)
        wv_sb = sb("wv_sb", [P, DH, D], F32, wl)
        wo_sb = sb("wo_sb", [P, DH, D], F32, wl)
        woT = sb("woT", [P, DH, D], F32, wl)
        fold = sb("fold", [P, DH, VW], F32, wl)
        bcol = sb("bcol", [P, 3, DH], F32, wl)
        bbc = sb("bbc", [P, 2, DH, P], F32, wl)
        wt_sb = sb("wt_sb", [P, DH, PD], F32, wl)
        bt_row = sb("bt_row", [P, D], F32, wl)
        wl.close()
        V_hi = sb("V_hi", [P, 2 * NT, D], F32R, ph)
        V_lo = sb("V_lo", [P, 2 * NT, D], F32R, ph)
        PT_hi = sb("PT_hi", [P, NT, P], F32R, ph)
        PT_lo = sb("PT_lo", [P, NT, P], F32R, ph)
        G_hi = sb("G_hi", [P, DH, CW], F32R, ph)
        G_lo = sb("G_lo", [P, DH, CW], F32R, ph)
        A_hi = sb("A_hi", [P, DH, D], F32R, ph)
        A_lo = sb("A_lo", [P, DH, D], F32R, ph)
        WV_hi = sb("WV_hi", [P, DH, VW], F32R, ph)
        WV_lo = sb("WV_lo", [P, DH, VW], F32R, ph)
        probs = sb("probs", [P, NT * P], F32, ph)
        xn = sb("xn", [P, TC, D], F32, ph)
        vf = sb("vf", [P, 2, VW], F32, ph)
        v_bias = sb("v_bias", [P, VW], F32, ph)
        g_bias = sb("g_bias", [P, DH], F32, ph)
        posb = sb("posb", [P, NIT, D], F32, ph)
        wtT = sb("wtT", [PD, D], F32, ph)
        pst = sb("pst", [PD, CW], F32, ph)
        st1 = sb("st1", [P, TC, 6], F32, ph)
        mv1 = sb("mv1", [P, TC, 2], F32, ph)
        ve1 = sb("ve1", [P, TC], F32, ph)
        rs1 = sb("rs1", [P, TC], F32, ph)
        st2 = sb("st2", [P, TC, 6], F32, ph)
        mv2 = sb("mv2", [P, TC, 2], F32, ph)
        ve2 = sb("ve2", [P, TC], F32, ph)
        rs2 = sb("rs2", [P, TC], F32, ph)
        nm2 = sb("nm2", [P, TC], F32, ph)
        zs = sb("zs", [P, 2, D], F32, ph)
        x2t = sb("x2t", [P, D], F32, ph)
        smax = sb("smax", [P, TC, 6], F32, ph)
        mask = sb("mask", [P, NB * NT], F32, ph)
        q_zero = sb("q_zero", [P, 2], F32, ph)
        c_row = sb("c_row", [P, NB * NT], F32, ph)
        ph.close()

        ff = ExitStack()
        small = sb("small", [NB, 16, NE], F32, ff)
        top_i = sb("top_i", [NB, NE], U32, ff)
        diag_w = sb("diag_w", [NB, NB, TOPK], F32, ff)
        meanT = sb("meanT", [P, DH, NB], F32, ff)
        gamma_row = sb("gamma_row", [P, D], F32, ff)
        beta_row = sb("beta_row", [P, D], F32, ff)
        xf_hi = sb("xf_hi", [P, DH, CW], F32R, ff)
        xf_lo = sb("xf_lo", [P, DH, CW], F32R, ff)
        h_hi = sb("h_hi", [P, TOPK * FQ, CW], F32R, ff)
        h_lo = sb("h_lo", [P, TOPK * FQ, CW], F32R, ff)
        w1_hi = sb("w1_hi", [P, TOPK, DH, F], F32R, ff)
        w1_lo = sb("w1_lo", [P, TOPK, DH, F], F32R, ff)
        w2_hi = sb("w2_hi", [P, TOPK, FQ, D], F32R, ff)
        w2_lo = sb("w2_lo", [P, TOPK, FQ, D], F32R, ff)
        w1_raw = sb("w1_raw", [P, TOPK, DH, F], F32, ff)
        w2_raw = sb("w2_raw", [P, TOPK, FQ, D], F32, ff)
        b2_raw = sb("b2_raw", [P, TOPK, D], F32, ff)
        b1_sb = sb("b1_sb", [P, NB * TOPK * FQ], F32, ff)
        b1_cur = sb("b1_cur", [P, NF], F32, ff)
        w_cur = sb("w_cur", [P, TOPK], F32, ff)
        b2_sum = sb("b2_sum", [P, D], F32, ff)
        gel = sb("gel", [P, 4, CW], F32, ff)
        x2s = sb("x2s", [P, TC, D], F32, ff)
        x2b = sb("x2b", [P, TC, D], F32, ff)
        yb = sb("yb", [P, TC, D], F32, ff)
        ob = sb("ob", [P, TC, D], F32, ff)
        st3 = sb("st3", [P, TC, 6], F32, ff)
        mv3 = sb("mv3", [P, TC, 2], F32, ff)
        ve3 = sb("ve3", [P, TC], F32, ff)
        rs3 = sb("rs3", [P, TC], F32, ff)
        ff.close()

        ps = ctx.enter_context(nc.psum_tensor("ps", [P, 8, 512], F32))
        scores = ps[:, 0:3, 0:SW]
        T0, T1, T2, AUX, OB = 3, 4, 5, 6, 7
        TB = (T0, T1, T2)

        ld_w = sem("ld_w")
        ld_img = sem("ld_img")
        ld_txt = sem("ld_txt")
        ld_pos = sem("ld_pos")
        ld_rows = sem("ld_rows")
        ld_ffn = sem("ld_ffn")
        c_ident = sem("c_ident")
        c_zero = sem("c_zero")
        su_pe = sem("su_pe")
        su_v = sem("su_v")
        su_wot = sem("su_wot")
        su_wtt = sem("su_wtt")
        su_bbc = sem("su_bbc")
        su_done = sem("su_done")
        im_dve = sem("im_dve")
        im_act = sem("im_act")
        pt_ready = sem("pt_ready")
        pt_even = sem("pt_even")
        pt_odd = sem("pt_odd")
        pst_ready = sem("pst_ready")
        h_ready = sem("h_ready")
        h_done = sem("h_done")
        st1_done = sem("st1_done")
        mv1_done = sem("mv1_done")
        ve1_done = sem("ve1_done")
        rs1_done = sem("rs1_done")
        xn_ready = sem("xn_ready")
        zb_ready = sem("zb_ready")
        xt_ready = sem("xt_ready")
        xt_hi = sem("xt_hi")
        xt_lo = sem("xt_lo")
        xt_copied = sem("xt_copied")
        v_ready = sem("v_ready")
        v_f = sem("v_f")
        v_hi = sem("v_hi")
        v_lo = sem("v_lo")
        v_info = sem("v_info")
        g_ready = sem("g_ready")
        g_hi = sem("g_hi")
        g_lo = sem("g_lo")
        s_ready = sem("s_ready")
        max_done = sem("max_done")
        full_max = sem("full_max")
        shift_done = sem("shift_done")
        exp_done = sem("exp_done")
        t_ready = sem("t_ready")
        t_hi = sem("t_hi")
        t_lo = sem("t_lo")
        o_ready = sem("o_ready")
        rinv_done = sem("rinv_done")
        km_done = sem("km_done")
        rs_done = sem("rs_done")
        o_done = sem("o_done")
        st2_done = sem("st2_done")
        mv2_done = sem("mv2_done")
        ve2_done = sem("ve2_done")
        rs2_done = sem("rs2_done")
        nmr2_done = sem("nmr2_done")
        x2_done = sem("x2_done")
        acc_done = sem("acc_done")
        r_pe = sem("r_pe")
        r_v = sem("r_v")
        r_a = sem("r_a")
        r_idx = sem("r_idx")
        w1_in = sem("w1_in")
        w2_in = sem("w2_in")
        b1_in = sem("b1_in")
        b2_in = sem("b2_in")
        w1_hid = sem("w1_hid")
        w1_lod = sem("w1_lod")
        w2_hid = sem("w2_hid")
        w2_lod = sem("w2_lod")
        cur_done = sem("cur_done")
        b2_half = sem("b2_half")
        b2_done = sem("b2_done")
        z_back = sem("z_back")
        kept2 = sem("kept2")
        x2s_ready = sem("x2s_ready")
        zbeta = sem("zbeta")
        x2b_ready = sem("x2b_ready")
        xf_ready = sem("xf_ready")
        xf_hid = sem("xf_hid")
        xf_lod = sem("xf_lod")
        f_ready = sem("f_ready")
        gelu_done = sem("gelu_done")
        h_hid = sem("h_hid")
        h_lod = sem("h_lod")
        y_ready = sem("y_ready")
        y_done = sem("y_done")
        st3_done = sem("st3_done")
        mv3_done = sem("mv3_done")
        ve3_done = sem("ve3_done")
        rs3_done = sem("rs3_done")
        nrm_done = sem("nrm_done")
        gam_done = sem("gam_done")
        out_ready = sem("out_ready")
        stored = [sem(f"stored{j}") for j in range(TC)]

        XB, Y0 = 4, 5

        def batches(eng, body):
            with eng.Fori(0, NB - 1) as b:
                for c in range(NC):
                    body(b, c, True)
            for c in range(NC):
                body(NB - 1, c, False)

        def width(c):
            return LASTW if c == NC - 1 else CW

        def nrows(c, j):
            return LASTR if c == NC - 1 and j == TC - 1 else P

        def nxt(b, c):
            return (b + 1, 0) if c == NC - 1 else (b, c + 1)

        def wait_apart(eng, counter, value):
            eng.wait_ge(counter, value)
            eng.sem_inc(waits_apart, 1)

        def z_at(t, r):
            return Z[0:r, bass.ds(t, 1), :].rearrange("p o d -> p (o d)")

        def v_at(V, b, t, r):
            return V[0:r, bass.ds((b % 2) * NT + t, 1), :].rearrange("p o d -> p (o d)")

        def patches(b, lo=0, n=NIMG):
            first = b * NT + NIT // 2
            return Z[0:PD, bass.ds(first, NIT // 2), :].rearrange("p t d -> p (t d)")[:, lo:lo + n]

        def xT_at(X, b, h, lo, n):
            return X[:, bass.ds(b % 2, 1), h, lo:lo + n].rearrange("p o n -> p (o n)")

        def xt_psum(bank, r):
            return ps[:, bank, 0:DH * P].rearrange("p (h t) -> p h t", h=DH)[:, :, 0:r]

        def image_views(g):
            return (imp[:, g].rearrange("p j (r k) -> p j r k", r=PATCH),
                    img[:, g, :].rearrange("p (r j k) -> p j r k", r=PATCH, j=SIDE))

        def patch_views(g):
            src = ps[0:PD, g % 4, :].rearrange("p (j b i) -> p b i j", j=4, b=NB // 2)
            b0 = (g // GPI) * 4
            return [(patches(b0 + b).rearrange("p (i j) -> p i j", j=SIDE)[:, :, (g % GPI) * 4:(g % GPI) * 4 + 4],
                     src[:, b]) for b in range(4)]

        waits_apart = sem("waits_apart")

        block = ctx.enter_context(nc.Block())

        @block.sync
        def _(sp):
            for g in range(2):
                sp.dma_start(img[:, g, :], x[4 * g:4 * g + 4, 0].rearrange("b (i r) w -> (b i) (r w)", r=PATCH)
                             ).then_inc(ld_img, 16)
            for w_dram, w_sb in ((Wq, wq_sb), (Wk, wk_sb), (Wv, wv_sb), (Wo, wo_sb)):
                sp.dma_start(w_sb[:], w_dram.rearrange("(h p) d -> p h d", p=P)).then_inc(ld_w, 16)
            sp.dma_start(wt_sb[:], Wt.rearrange("(h p) k -> p h k", p=P)).then_inc(ld_w, 16)
            with nc.allow_non_contiguous_dma("three bias vectors laid on partitions, once"):
                for n, b_dram in enumerate((bq, bk, bv)):
                    sp.dma_start(bcol[:, n, :], b_dram.rearrange("(h p) -> p h", p=P)).then_inc(ld_w, 16)
            sp.dma_start(bt_row[:], bt.partition_broadcast(P)).then_inc(ld_w, 16)
            sp.dma_start(v_bias[:, D:D + 1], bq[0:1].partition_broadcast(P)).then_inc(ld_w, 16)
            sp.dma_start(v_bias[:, D + 1:D + 2], bk[0:1].partition_broadcast(P)).then_inc(ld_w, 16)
            sp.dma_start(posb[:], pos[0].rearrange("(t p) d -> p t d", p=P)).then_inc(ld_w, 16)
            sp.dma_start(Z[0:NTXT, :, :].rearrange("p (b t) d -> p b t d", t=NT)[:, :, NT - 1, :],
                         txt.rearrange("b p d -> p b d")).then_inc(ld_txt, 16)
            sp.dma_start(bo_row[:], bo.partition_broadcast(P)).then_inc(ld_rows, 16)
            sp.dma_start(br_row[:], br.partition_broadcast(NB)).then_inc(ld_rows, 16)
            sp.dma_start(wr_sb[:], Wr.rearrange("(h p) e -> p h e", p=P)).then_inc(ld_rows, 16)

            sp.wait_ge(r_v, 16)
            sp.dma_start(route_i[:], top_i[:, 0:TOPK].bitcast(I32)).then_inc(r_idx, 16)
            sp.wait_ge(r_idx, 16)

            def load_experts(b):
                for k in range(TOPK):
                    e = sp.value_load(route_i[0:1, bass.ds(b * TOPK + k, 1)], min_val=0, max_val=NE - 1)
                    sp.dma_start(w1_raw[:, k], W1[bass.ds(e, 1)].rearrange("o (h p) f -> p (o h) f", p=P)
                                 ).then_inc(w1_in, 16)
                    with nc.allow_non_contiguous_dma("an expert's bias laid on partitions"):
                        sp.dma_start(b1_sb[:, bass.ds((b * TOPK + k) * FQ, FQ)],
                                     b1[bass.ds(e, 1)].rearrange("o (q p) -> p (o q)", p=P)).then_inc(b1_in, 16)
                    sp.dma_start(w2_raw[:, k], W2[bass.ds(e, 1)].rearrange("o (q p) d -> p (o q) d", p=P)
                                 ).then_inc(w2_in, 16)
                    sp.dma_start(b2_raw[:, k], b2[bass.ds(e, 1)].rearrange("o d -> (o d)").partition_broadcast(P)
                                 ).then_inc(b2_in, 16)

            sp.dma_start(gamma_row[:], gamma.partition_broadcast(P)).then_inc(ld_ffn, 16)
            sp.dma_start(beta_row[:], beta.partition_broadcast(P)).then_inc(ld_ffn, 16)
            load_experts(0)

            def store(b, c, has_next):
                if c == 0 and has_next:
                    sp.wait_ge(w1_lod, b + 1)
                    sp.wait_ge(w2_lod, b + 1)
                    sp.wait_ge(b2_done, b + 1)
                    load_experts(b + 1)
                for j in range(TC):
                    r = nrows(c, j)
                    sp.wait_ge(out_ready, b * NT + c * TC + j + 1)
                    sp.dma_start(out[bass.ds(b, 1), c * CW + j * P:c * CW + j * P + r, :].rearrange("o p d -> (o p) d"),
                                 ob[0:r, j, :]).then_inc(stored[j], 16)

            batches(sp, store)
            for j in range(TC):
                sp.wait_ge(stored[j], 16 * (1 + NB * NC))

        @block.gpsimd
        def _(pool):
            pool.memset(ones[:], 1.0).then_inc(c_zero, 1)
            pool.memset(half_neg[:], -0.5).then_inc(c_zero, 1)
            pool.memset(probs[:, S:], 0.0).then_inc(c_zero, 1)
            pool.memset(mv1[:], 0.0).then_inc(c_zero, 1)
            pool.memset(x2t[:], 0.0).then_inc(x2_done, 2)
            pool.memset(acc[:], 0.0).then_inc(c_zero, 1)
            for X in (xT_hi, xT_lo):
                for par in range(2):
                    pool.memset(X[:, par, :, S:SE].bitcast(F32), 0.0).then_inc(c_zero, 1)
            pool.wait_ge(c_zero, 1)
            pool.affine_select(out=ident[:], in_=ones[:], compare_op=ALU.is_equal, fill=0.0, base=0,
                               pattern=[[-1, P]], channel_multiplier=1).then_inc(c_ident, 1)

            def ln1_and_bo(b, c):
                t = b * NT + c * TC
                wait_apart(pool, mv1_done, t + TC)
                pool.tensor_scalar(ve1[:], mv1[:, :, 1], EPS, None, ALU.add).then_inc(ve1_done, 1)
                pool.wait_ge(ve1_done, b * NC + c + 1)
                pool.tensor_tensor(rs1[:], ve1[:], half_neg[:], ALU.pow).then_inc(rs1_done, 1)
                for j in range(TC):
                    r = nrows(c, j)
                    wait_apart(pool, xn_ready, t + j + 1)
                    pool.tensor_tensor(z_at(t + j, r), z_at(t + j, r), bo_row[0:r, :], ALU.add).then_inc(zb_ready, 1)

            def ln2_sum(b, c, j):
                r = nrows(c, j)
                t = b * NT + c * TC + j
                k = (c * TC + j) % 2
                wait_apart(pool, mv2_done, t + 1)
                pool.tensor_scalar(ve2[0:r, j:j + 1], mv2[0:r, j, 1:2], EPS, None, ALU.add).then_inc(ve2_done, 1)
                pool.wait_ge(ve2_done, t + 1)
                pool.tensor_tensor(rs2[0:r, j:j + 1], ve2[0:r, j:j + 1], half_neg[0:r, 0:1], ALU.pow
                                   ).then_inc(rs2_done, 1)
                wait_apart(pool, rs2_done, t + 1)
                pool.tensor_scalar(nm2[0:r, j:j + 1], mv2[0:r, j, 0:1], rs2[0:r, j:j + 1], -1.0,
                                   ALU.mult, ALU.mult).then_inc(nmr2_done, 1)
                pool.tensor_copy(rstd2[0:r, bass.ds(t, 1)], rs2[0:r, j:j + 1]).then_inc(kept2, 1)
                wait_apart(pool, nmr2_done, t + 1)
                pool.tensor_copy(nmr2[0:r, bass.ds(t, 1)], nm2[0:r, j:j + 1]).then_inc(kept2, 1)
                pool.tensor_scalar(x2t[0:r, :], zs[0:r, k, :], rs2[0:r, j:j + 1], nm2[0:r, j:j + 1],
                                   ALU.mult, ALU.add).then_inc(x2_done, 1)
                wait_apart(pool, x2_done, 2 + t + 1)
                a = acc[0:r, bass.ds(b, 1), :].rearrange("p o d -> p (o d)")
                pool.tensor_tensor(a, a, x2t[0:r, :], ALU.add).then_inc(acc_done, 1)

            pool.wait_ge(c_zero, 9)
            pool.wait_ge(ld_rows, 16 * 3)
            for c in range(NC):
                ln1_and_bo(0, c)

            def body(b, c, has_next):
                if has_next:
                    ln1_and_bo(b + 1, c)
                ln2_sum(b, c, 0)
                ln2_sum(b, c, 1)
                ln2_sum(b, c, 2)

            batches(pool, body)

            def add_beta(b, c):
                t = b * NT + c * TC
                for j in range(TC):
                    r = nrows(c, j)
                    wait_apart(pool, x2s_ready, t + j + 1)
                    pool.tensor_tensor(z_at(t + j, r), z_at(t + j, r), beta_row[0:r, :], ALU.add).then_inc(zbeta, 1)

            def make_x2b(b, c):
                wait_apart(pool, b2_done, b + 1)
                for j in range(TC):
                    r = nrows(c, j)
                    pool.tensor_tensor(x2b[0:r, j, :], x2s[0:r, j, :], b2_sum[0:r, :], ALU.add
                                       ).then_inc(x2b_ready, 1)

            pool.wait_ge(ld_ffn, 32)
            for j in range(TC):
                pool.memset(ve3[:, j:j + 1], 1.0).then_inc(stored[j], 16)
            add_beta(0, 0)
            make_x2b(0, 0)

            def ffn(b, c, has_next):
                t = b * NT + c * TC
                more = has_next or c < NC - 1
                if more:
                    add_beta(*nxt(b, c))
                for j in range(TC):
                    r = nrows(c, j)
                    wait_apart(pool, mv3_done, t + j + 1)
                    pool.tensor_scalar(ve3[0:r, j:j + 1], mv3[0:r, j, 1:2], EPS, None, ALU.add).then_inc(ve3_done, 1)
                    pool.wait_ge(ve3_done, t + j + 1)
                    pool.tensor_tensor(rs3[0:r, j:j + 1], ve3[0:r, j:j + 1], half_neg[0:r, 0:1], ALU.pow
                                       ).then_inc(rs3_done, 1)
                for j in range(TC):
                    r = nrows(c, j)
                    pool.wait_ge(gam_done, t + j + 1)
                    wait_apart(pool, stored[j], 16 * (b * NC + c + 1))
                    pool.tensor_tensor(ob[0:r, j, :], yb[0:r, j, :], z_at(t + j, r), ALU.add).then_inc(out_ready, 1)
                if more:
                    make_x2b(*nxt(b, c))

            batches(pool, ffn)

        @block.scalar
        def _(act):
            act.wait_ge(ld_img, 32)
            act.activation(*image_views(1), ACT.Copy).then_inc(im_act, 1)
            for g in range(1, NPG, 2):
                act.wait_ge(pt_ready, g + 1)
                for dst, src in patch_views(g):
                    ins = act.activation(dst, src, ACT.Copy)
                ins.then_inc(pt_odd, 1)

            def stage_patches(b, c):
                n = width(c) - NTXT if c == NC - 1 else CW
                act.activation(pst[:, 0:n], patches(b, c * CW, n), ACT.Copy).then_inc(pst_ready, 1)

            def split_xt(b, c, j, bank):
                r = nrows(c, j)
                act.wait_ge(xt_ready, b * NT + c * TC + j + 1)
                act.activation(xs_hi[:, :, j * P:j * P + r], xt_psum(bank, r), ACT.Copy).then_inc(xt_hi, 1)

            def split_v(b, c, j):
                r = nrows(c, j)
                wait_apart(act, v_f, b * NT + c * TC + j + 1)
                act.activation(v_at(V_hi, b, c * TC + j, r), vf[0:r, j % 2, 0:D], ACT.Copy).then_inc(v_hi, 1)

            def split_g(b, c):
                w = width(c)
                for h, bank in ((0, T2), (1, AUX)):
                    act.wait_ge(g_ready, DH * (b * NC + c) + h + 1)
                    act.activation(G_hi[:, h, 0:w], ps[:, bank, 0:w], ACT.Identity, bias=g_bias[:, h:h + 1]
                                   ).then_inc(g_hi, 1)

            def exp_tile(b, c, j):
                r = nrows(c, j)
                act.wait_ge(shift_done, b * NT + c * TC + j + 1)
                act.activation(probs[0:r, 0:S].rearrange("p (a b) -> p a b", b=SW), scores[0:r], ACT.Exp, bias=smax[0:r, j, 2:3], scale=SCALE,
                               accum_out=smax[0:r, j, 3:4]).then_inc(exp_done, 1)

            act.wait_ge(su_done, 1)
            act.wait_ge(pt_even, NPG // 2)
            act.wait_ge(pt_odd, NPG // 2)
            for c in range(NC):
                if c:
                    act.wait_ge(h_ready, c * TC)
                stage_patches(0, c)
                if c:
                    act.wait_ge(xt_copied, 2 * c)
                for j, bank in ((0, AUX), (1, T0), (2, T1)):
                    split_xt(0, c, j, bank)
                for j in range(TC):
                    split_v(0, c, j)
            split_g(0, 0)
            act.wait_ge(c_zero, 9)
            exp_tile(0, 0, 0)

            def body(b, c, has_next):
                t = b * NT + c * TC
                more = has_next or c < NC - 1
                if has_next:
                    wait_apart(act, h_ready, (b + 1) * NIT + c * TC)
                    stage_patches(b + 1, c)
                for j in range(TC):
                    for u in range(NC):
                        act.wait_ge(t_ready, NC * (t + j) + u + 1)
                        act.activation(PT_hi[:, TC * u:TC * (u + 1), :].rearrange("p a b -> p (a b)"),
                                       ps[:, TB[u], 0:CW], ACT.Copy).then_inc(t_hi, 1)
                    if j < TC - 1:
                        exp_tile(b, c, j + 1)
                    elif more:
                        exp_tile(*nxt(b, c), 0)
                    if j == 0 and has_next:
                        act.wait_ge(xt_copied, 2 * ((b + 1) * NC + c))
                        split_xt(b + 1, c, 0, AUX)
                    if j == 1:
                        if has_next:
                            split_xt(b + 1, c, 1, T0)
                            split_xt(b + 1, c, 2, T1)
                        if more:
                            split_g(*nxt(b, c))
                        if has_next:
                            split_v(b + 1, c, 0)
                    if j == 2 and has_next:
                        split_v(b + 1, c, 1)
                        split_v(b + 1, c, 2)

            batches(act, body)

            for n, (need, dst, src, w) in enumerate(((4, 1, 0, NE), (12, 4, 3, NE), (17, 7, 6, TOPK))):
                act.wait_ge(r_v, need)
                act.activation(small[:, dst, 0:w], small[:, src, 0:w], ACT.Exp, bias=small[:, 9 + n, 0:1],
                               accum_out=small[:, 9 + n, 1:2]).then_inc(r_a, 1)

            def split_w1(b):
                act.wait_ge(w1_in, 16 * TOPK * (b + 1))
                act.activation(w1_hi[:].rearrange("p a b c -> p (a b c)"), w1_raw[:].rearrange("p a b c -> p (a b c)"),
                               ACT.Copy).then_inc(w1_hid, 1)

            def split_w2(b):
                act.wait_ge(w2_in, 16 * TOPK * (b + 1))
                for k in range(TOPK):
                    act.activation(w2_hi[:, k].rearrange("p a b -> p (a b)"), w2_raw[:, k].rearrange("p a b -> p (a b)"),
                                   ACT.Copy, scale=w_cur[:, k:k + 1]).then_inc(w2_hid, 1)

            def split_xf(b, c, h):
                w = width(c)
                act.wait_ge(xf_ready, DH * (b * NC + c) + h + 1)
                act.activation(xf_hi[:, h, 0:w], ps[:, XB, 0:w], ACT.Copy).then_inc(xf_hid, 1)

            act.wait_ge(r_v, 22)
            split_xf(0, 0, 0)
            split_xf(0, 0, 1)
            split_w1(0)

            def ffn(b, c, has_next):
                n = NF * (b * NC + c)
                w = width(c)
                if c == 0:
                    wait_apart(act, b1_in, 16 * TOPK * (b + 1))
                    act.activation(b1_cur[:], b1_sb[:, bass.ds(b * NF, NF)], ACT.Copy).then_inc(cur_done, 1)
                    act.activation(w_cur[:], route_w[:, bass.ds(b * TOPK, TOPK)], ACT.Copy).then_inc(cur_done, 1)
                    act.wait_ge(cur_done, 2 * (b + 1))
                for f in range(NF):
                    act.wait_ge(f_ready, n + f + 1)
                    act.wait_ge(h_lod, n + f + 1)
                    act.activation(gel[:, f % 4, 0:w], ps[:, f % 4, 0:w], ACT.Gelu,
                                   bias=b1_cur[:, f:f + 1]).then_inc(gelu_done, 1)
                    if c == 0 and f == 1:
                        split_w2(b)
                if c == NC - 1 and has_next:
                    split_w1(b + 1)
                if has_next or c < NC - 1:
                    split_xf(*nxt(b, c), 0)
                    split_xf(*nxt(b, c), 1)

            batches(act, ffn)

        @block.vector
        def _(dve):
            dve.wait_ge(ld_img, 32)
            dve.tensor_copy(*image_views(0)).then_inc(im_dve, 1)
            for g in range(0, NPG, 2):
                dve.wait_ge(pt_ready, g + 1)
                for dst, src in patch_views(g):
                    ins = dve.tensor_copy(dst, src)
                ins.then_inc(pt_even, 1)

            step = [0]

            def link(ins):
                step[0] += 1
                ins.then_inc(su_v, 1)
                dve.wait_ge(su_v, step[0])

            dve.wait_ge(ld_w, 16 * 12)
            dve.wait_ge(c_zero, 9)
            for n, which in enumerate((0, 2)):
                for h in range(DH):
                    ins = dve.tensor_scalar(bbc[:, n, h, :], ones[:], bcol[:, which, h:h + 1], None, ALU.mult)
                    link(ins)
            dve.memset(fold[:], 0.0).then_inc(su_bbc, 1)
            dve.wait_ge(su_pe, 1)
            dve.tensor_copy(woT[:].rearrange("p h d -> p (h d)"), ps[:, 4, :]).then_inc(su_wot, 1)
            dve.wait_ge(su_pe, 2)
            dve.tensor_copy(wtT[:], ps[0:PD, 5, 0:D]).then_inc(su_wtt, 1)
            dve.wait_ge(su_pe, 3)
            a2 = "p h d -> p (h d)"
            link(dve.tensor_copy(A_hi[:].rearrange(a2), ps[:, 6, :]))
            link(dve.tensor_tensor(A_lo[:].rearrange(a2), ps[:, 6, :], A_hi[:].rearrange(a2).bitcast(F32), ALU.subtract))
            dve.wait_ge(su_pe, 4)
            link(dve.tensor_copy(fold[:, :, 0:D], ps[:, 7, :].rearrange("p (h d) -> p h d", h=DH)))
            dve.wait_ge(su_pe, 5)
            link(dve.tensor_copy(fold[:, :, D:D + 3], ps[:, 5, 0:8].rearrange("p (h d) -> p h d", h=DH)[:, :, 0:3]))
            link(dve.tensor_copy(g_bias[:], ps[:, 5, 16:16 + DH]))
            link(dve.tensor_copy(WV_hi[:], fold[:]))
            link(dve.tensor_tensor(WV_lo[:], fold[:], WV_hi[:].bitcast(F32), ALU.subtract))
            dve.wait_ge(su_pe, 6)
            link(dve.tensor_copy(v_bias[:, 0:D], ps[:, 4, 0:D]))
            link(dve.tensor_copy(v_bias[:, D + 2:D + 3], ps[:, 4, D:D + 1]))
            link(dve.memset(v_bias[:, D + 3:VW], 0.0))
            dve.tensor_tensor(posb[:], posb[:], bt_row[:].unsqueeze(1).to_broadcast([P, NIT, D]), ALU.add
                              ).then_inc(su_done, 1)
            dve.wait_ge(su_done, 1)
            dve.wait_ge(ld_txt, 16)

            def tokens(b, c, j, bank):
                t = b * NT + c * TC + j
                r = nrows(c, j)
                T = c * TC + j
                if T < NIT:
                    dve.wait_ge(h_ready, b * NIT + T + 1)
                    dve.tensor_tensor(z_at(t, P), ps[:, bank, 0:D], posb[:, T, :], ALU.add).then_inc(h_done, 1)
                    wait_apart(dve, h_done, b * NIT + T + 1)
                dve.bn_stats(st1[0:r, j, :], z_at(t, r)).then_inc(st1_done, 1)
                wait_apart(dve, st1_done, t + 1)
                dve.bn_aggr(mv1[0:r, j, :], st1[0:r, j, :]).then_inc(mv1_done, 1)

            def normal1(b, c):
                t = b * NT + c * TC
                dve.wait_ge(rs1_done, b * NC + c + 1)
                for j in range(TC):
                    r = nrows(c, j)
                    dve.tensor_scalar(xn[0:r, j, :], z_at(t + j, r), mv1[0:r, j, 0:1], rs1[0:r, j:j + 1],
                                      ALU.subtract, ALU.mult).then_inc(xn_ready, 1)

            def low_xt(b, c, j, bank):
                r = nrows(c, j)
                s = slice(j * P, j * P + r)
                dve.wait_ge(xt_hi, b * NT + c * TC + j + 1)
                dve.tensor_tensor(xs_lo[:, :, s], xt_psum(bank, r), xs_hi[:, :, s].bitcast(F32), ALU.subtract
                                  ).then_inc(xt_lo, 1)

            def copy_xT(b, c):
                n = width(c)
                dve.wait_ge(xt_lo, b * NT + c * TC + TC)
                for src, dst in ((xs_hi, xT_hi), (xs_lo, xT_lo)):
                    dve.tensor_copy(dst[:, bass.ds(b % 2, 1), :, c * CW:c * CW + n].rearrange("p o h n -> p (o h) n"),
                                    src[:, :, 0:n]).then_inc(xt_copied, 1)

            def value_sum(b, c, j, bank):
                r = nrows(c, j)
                t = b * NT + c * TC + j
                used = 3 * (t if j == 0 else t - 1)
                if type(used) is not int or used > 0:
                    dve.wait_ge(v_info, used)
                dve.wait_ge(v_ready, t + 1)
                dve.tensor_tensor(vf[0:r, j % 2, :], ps[0:r, bank, 0:VW], v_bias[0:r, :], ALU.add).then_inc(v_f, 1)

            def low_v(b, c, j):
                t = b * NT + c * TC + j
                r = nrows(c, j)
                dve.wait_ge(v_hi, t + 1)
                dve.tensor_tensor(v_at(V_lo, b, c * TC + j, r), vf[0:r, j % 2, 0:D], v_at(V_hi, b, c * TC + j, r).bitcast(F32),
                                  ALU.subtract).then_inc(v_lo, 1)
                qz = q_zero[0:r, j % 2:j % 2 + 1]
                dve.tensor_scalar(qz, vf[0:r, j % 2, D:D + 1], 0.0, None, ALU.not_equal).then_inc(v_info, 1)
                dve.tensor_copy(c_row[0:r, bass.ds(t, 1)], vf[0:r, j % 2, D + 2:D + 3]).then_inc(v_info, 1)
                dve.wait_ge(v_info, 3 * t + 2)
                dve.tensor_scalar(mask[0:r, bass.ds(t, 1)], vf[0:r, j % 2, D + 1:D + 2], 0.0, qz, ALU.not_equal, ALU.mult
                                  ).then_inc(v_info, 1)

            def low_g(b, c):
                w = width(c)
                for h, bank in ((0, T2), (1, AUX)):
                    dve.wait_ge(g_hi, DH * (b * NC + c) + h + 1)
                    dve.scalar_tensor_tensor(out=G_lo[:, h, 0:w], in0=ps[:, bank, 0:w], scalar=g_bias[:, h:h + 1],
                                             in1=G_hi[:, h, 0:w].bitcast(F32), op0=ALU.add, op1=ALU.subtract
                                             ).then_inc(g_lo, 1)

            def shift(b, c, j):
                t = b * NT + c * TC + j
                r = nrows(c, j)
                cr = c_row[0:r, bass.ds(t, 1)]
                dve.wait_ge(v_info, 3 * (t + 1))
                dve.wait_ge(s_ready, t + 1)
                dve.reduce_max(smax[0:r, j, 0:1], scores[0:r], AX_XY).then_inc(max_done, 1)
                dve.wait_ge(max_done, t + 1)
                dve.tensor_tensor(smax[0:r, j, 1:2], smax[0:r, j, 0:1], cr, ALU.add).then_inc(full_max, 1)
                dve.wait_ge(full_max, t + 1)
                dve.tensor_scalar(smax[0:r, j, 2:3], cr, smax[0:r, j, 1:2], SCALE, ALU.subtract, ALU.mult
                                  ).then_inc(shift_done, 1)

            def finish(b, c, j):
                t = b * NT + c * TC + j
                r = nrows(c, j)
                dve.wait_ge(exp_done, t + 1)
                dve.reciprocal(smax[0:r, j, 4:5], smax[0:r, j, 3:4]).then_inc(rinv_done, 1)
                dve.wait_ge(rinv_done, t + 1)
                dve.tensor_tensor(smax[0:r, j, 5:6], mask[0:r, bass.ds(t, 1)], smax[0:r, j, 4:5], ALU.mult
                                  ).then_inc(rs_done, 1)
                dve.wait_ge(rs_done, t + 1)
                dve.wait_ge(zb_ready, t + 1)
                T = c * TC + j
                dve.wait_ge(x2_done, 2 + t - (T > 0))
                dve.wait_ge(o_ready, t + 1)
                dve.scalar_tensor_tensor(out=zs[0:r, T % 2, :], in0=ps[0:r, OB, 0:D], scalar=smax[0:r, j, 5:6],
                                         in1=z_at(t, r), op0=ALU.mult, op1=ALU.add).then_inc(o_done, 1)
                dve.wait_ge(o_done, t + 1)
                dve.bn_stats(st2[0:r, j, :], zs[0:r, T % 2, :]).then_inc(st2_done, 1)
                dve.tensor_copy(z_at(t, r), zs[0:r, T % 2, :]).then_inc(z_back, 1)
                wait_apart(dve, st2_done, t + 1)
                dve.bn_aggr(mv2[0:r, j, :], st2[0:r, j, :]).then_inc(mv2_done, 1)

            for c in range(NC):
                for j, bank in ((0, AUX), (1, T0), (2, T1)):
                    tokens(0, c, j, bank)
                normal1(0, c)
                for j, bank in ((0, AUX), (1, T0), (2, T1)):
                    low_xt(0, c, j, bank)
                copy_xT(0, c)
                value_sum(0, c, 0, T2)
                value_sum(0, c, 1, AUX)
                low_v(0, c, 0)
                value_sum(0, c, 2, T0)
                low_v(0, c, 1)
                low_v(0, c, 2)
            low_g(0, 0)
            shift(0, 0, 0)

            def body(b, c, has_next):
                t = b * NT + c * TC
                more = has_next or c < NC - 1
                for j in range(TC):
                    for u in range(NC):
                        dve.wait_ge(t_hi, NC * (t + j) + u + 1)
                        s = slice(TC * u, TC * (u + 1))
                        dve.tensor_tensor(PT_lo[:, s, :].rearrange("p a b -> p (a b)"), ps[:, TB[u], 0:CW],
                                          PT_hi[:, s, :].rearrange("p a b -> p (a b)").bitcast(F32), ALU.subtract
                                          ).then_inc(t_lo, 1)
                    if j < TC - 1:
                        shift(b, c, j + 1)
                    elif more:
                        shift(*nxt(b, c), 0)
                    if j == 0 and has_next:
                        for i, bank in ((0, AUX), (1, T0), (2, T1)):
                            tokens(b + 1, c, i, bank)
                        normal1(b + 1, c)
                    if j == 1:
                        if has_next:
                            low_xt(b + 1, c, 1, T0)
                            low_xt(b + 1, c, 2, T1)
                            copy_xT(b + 1, c)
                        if more:
                            low_g(*nxt(b, c))
                    if j == 2 and has_next:
                        value_sum(b + 1, c, 1, T0)
                        value_sum(b + 1, c, 2, T1)
                        low_v(b + 1, c, 1)
                        low_v(b + 1, c, 2)
                    finish(b, c, j)
                    if j == 0 and has_next:
                        low_xt(b + 1, c, 0, AUX)
                    if j == 1 and has_next:
                        value_sum(b + 1, c, 0, AUX)
                        low_v(b + 1, c, 0)

            batches(dve, body)

            rstep = [0]

            def rlink(ins):
                rstep[0] += 1
                ins.then_inc(r_v, 1)
                dve.wait_ge(r_v, rstep[0])

            sm = lambda i: small[:, i, :]
            dve.wait_ge(r_pe, 1)
            rlink(dve.tensor_scalar(meanT[:], ps[:, 0, 0:DH * NB].rearrange("p (h b) -> p h b", h=DH), 1.0 / S, None,
                                    ALU.mult))
            dve.wait_ge(r_pe, 2)
            rlink(dve.tensor_tensor(sm(0), ps[0:NB, 1, 0:NE], br_row[:], ALU.add))
            rlink(dve.reduce_max(small[:, 9, 2:3], sm(0), AX_X))
            rlink(dve.tensor_scalar(small[:, 9, 0:1], small[:, 9, 2:3], -1.0, None, ALU.mult))
            dve.wait_ge(r_a, 1)
            rlink(dve.reciprocal(small[:, 9, 3:4], small[:, 9, 1:2]))
            rlink(dve.tensor_scalar(sm(2), sm(1), small[:, 9, 3:4], None, ALU.mult))
            dve.wait_ge(r_pe, 3)
            rlink(dve.tensor_scalar(sm(5), ps[0:NB, 2, 0:NE], float(S), None, ALU.mult))
            rlink(dve.reciprocal(sm(8), sm(5)))
            rlink(dve.tensor_scalar(sm(12), sm(8), CAPACITY, 1.0, ALU.mult, ALU.min))
            rlink(dve.tensor_tensor(sm(3), sm(2), sm(12), ALU.mult))
            rlink(dve.reduce_max(small[:, 10, 2:3], sm(3), AX_X))
            rlink(dve.tensor_scalar(small[:, 10, 0:1], small[:, 10, 2:3], -1.0, None, ALU.mult))
            dve.wait_ge(r_a, 2)
            rlink(dve.reciprocal(small[:, 10, 3:4], small[:, 10, 1:2]))
            rlink(dve.tensor_scalar(sm(13), sm(4), small[:, 10, 3:4], None, ALU.mult))
            rlink(dve.max(sm(6), sm(13)))
            rlink(dve.max_index(top_i[:], sm(6), sm(13)))
            rlink(dve.tensor_scalar(small[:, 11, 0:1], small[:, 6, 0:1], -1.0, None, ALU.mult))
            dve.wait_ge(r_a, 3)
            rlink(dve.reciprocal(small[:, 11, 3:4], small[:, 11, 1:2]))
            rlink(dve.tensor_scalar(small[:, 14, 0:TOPK], small[:, 7, 0:TOPK], small[:, 11, 3:4], None, ALU.mult))
            for k in range(TOPK):
                rlink(dve.tensor_scalar(diag_w[:, :, k], ident[0:NB, 0:NB], small[:, 14, k:k + 1], None, ALU.mult))
            dve.wait_ge(r_pe, 4)
            rlink(dve.tensor_copy(route_w[:], ps[:, 3, 0:NB * TOPK]))

            def low_w1(b):
                dve.wait_ge(w1_hid, b + 1)
                v = "p a b c -> p (a b c)"
                dve.tensor_tensor(w1_lo[:].rearrange(v), w1_raw[:].rearrange(v), w1_hi[:].rearrange(v).bitcast(F32),
                                  ALU.subtract).then_inc(w1_lod, 1)

            def low_w2(b):
                for k in range(TOPK):
                    dve.wait_ge(w2_hid, TOPK * b + k + 1)
                    v = "p a b -> p (a b)"
                    ins = dve.scalar_tensor_tensor(
                        out=w2_lo[:, k].rearrange(v), in0=w2_raw[:, k].rearrange(v),
                        scalar=route_w[:, bass.ds(b * TOPK + k, 1)], in1=w2_hi[:, k].rearrange(v).bitcast(F32),
                        op0=ALU.mult, op1=ALU.subtract)
                ins.then_inc(w2_lod, 1)

            def sum_b2(b):
                dve.wait_ge(b2_in, 16 * TOPK * (b + 1))
                dve.tensor_scalar(b2_sum[:], b2_raw[:, 0, :], route_w[:, bass.ds(b * TOPK, 1)], None, ALU.mult
                                  ).then_inc(b2_half, 1)
                dve.wait_ge(b2_half, b + 1)
                dve.scalar_tensor_tensor(out=b2_sum[:], in0=b2_raw[:, 1, :], scalar=route_w[:, bass.ds(b * TOPK + 1, 1)],
                                         in1=b2_sum[:], op0=ALU.mult, op1=ALU.add).then_inc(b2_done, 1)

            def low_xf(b, c, h):
                w = width(c)
                dve.wait_ge(xf_hid, DH * (b * NC + c) + h + 1)
                dve.tensor_tensor(xf_lo[:, h, 0:w], ps[:, XB, 0:w], xf_hi[:, h, 0:w].bitcast(F32), ALU.subtract
                                  ).then_inc(xf_lod, 1)

            def ln3(b, c, j):
                t = b * NT + c * TC + j
                r = nrows(c, j)
                dve.wait_ge(x2b_ready, t + 1)
                dve.wait_ge(y_ready, t + 1)
                dve.tensor_tensor(yb[0:r, j, :], ps[0:r, Y0 + j, 0:D], x2b[0:r, j, :], ALU.add).then_inc(y_done, 1)
                dve.wait_ge(y_done, TC + t + 1)
                dve.bn_stats(st3[0:r, j, :], yb[0:r, j, :]).then_inc(st3_done, 1)
                wait_apart(dve, st3_done, t + 1)
                dve.bn_aggr(mv3[0:r, j, :], st3[0:r, j, :]).then_inc(mv3_done, 1)

            def norm3(b, c, j):
                t = b * NT + c * TC + j
                r = nrows(c, j)
                dve.wait_ge(rs3_done, t + 1)
                dve.tensor_scalar(yb[0:r, j, :], yb[0:r, j, :], mv3[0:r, j, 0:1], rs3[0:r, j:j + 1],
                                  ALU.subtract, ALU.mult).then_inc(nrm_done, 1)
                dve.wait_ge(nrm_done, t + 1)
                dve.tensor_tensor(yb[0:r, j, :], yb[0:r, j, :], gamma_row[0:r, :], ALU.mult).then_inc(gam_done, 1)

            def make_x2s(b, c, j):
                t = b * NT + c * TC + j
                r = nrows(c, j)
                dve.wait_ge(x2b_ready, b * NT + c * TC)
                dve.tensor_scalar(x2s[0:r, j, :], z_at(t, r), rstd2[0:r, bass.ds(t, 1)], nmr2[0:r, bass.ds(t, 1)],
                                  ALU.mult, ALU.add).then_inc(x2s_ready, 1)

            dve.wait_ge(kept2, 2 * NB * NT)
            for j in range(TC):
                dve.tensor_scalar(x2s[:, j, :], z_at(j, P), rstd2[:, j:j + 1], nmr2[:, j:j + 1], ALU.mult, ALU.add
                                  ).then_inc(x2s_ready, 1)
            dve.wait_ge(ld_ffn, 32)
            sum_b2(0)
            low_xf(0, 0, 0)
            low_xf(0, 0, 1)
            low_w1(0)
            dve.memset(st3[:, 0, :], 0.0).then_inc(h_lod, 4)
            dve.memset(st3[:, 1, :], 0.0).then_inc(y_done, TC)

            def ffn(b, c, has_next):
                n = NF * (b * NC + c)
                w = width(c)
                more = has_next or c < NC - 1
                for f in range(NF + 1):
                    if f < NF:
                        dve.wait_ge(gelu_done, n + f + 1)
                        dve.tensor_copy(h_hi[:, f, 0:w], gel[:, f % 4, 0:w]).then_inc(h_hid, 1)
                    if f:
                        g = f - 1
                        dve.wait_ge(h_hid, n + g + 1)
                        dve.tensor_tensor(h_lo[:, g, 0:w], gel[:, g % 4, 0:w], h_hi[:, g, 0:w].bitcast(F32),
                                          ALU.subtract).then_inc(h_lod, 1)
                    if c == 0 and f == 2:
                        low_w2(b)
                    if more and 3 <= f < 3 + TC:
                        make_x2s(*nxt(b, c), f - 3)
                if c == NC - 1 and has_next:
                    low_w1(b + 1)
                    dve.wait_ge(x2b_ready, NT * (b + 1))
                    sum_b2(b + 1)
                if more:
                    low_xf(*nxt(b, c), 0)
                ln3(b, c, 0)
                if more:
                    low_xf(*nxt(b, c), 1)
                ln3(b, c, 1)
                norm3(b, c, 0)
                ln3(b, c, 2)
                norm3(b, c, 1)
                norm3(b, c, 2)

            batches(dve, ffn)

        @block.tensor
        def _(pe):
            pe.wait_ge(c_ident, 1)
            for g in range(NPG):
                if g % GPI == 0:
                    pe.wait_ge(im_act if g else im_dve, 1)
                if g >= 4:
                    pe.wait_ge(pt_odd if g % 2 else pt_even, (g - 4) // 2 + 1)
                for k in range(4):
                    j = (g % GPI) * 4 + k
                    m = pe.transpose(ps[0:PD, g % 4, k * P:(k + 1) * P], imp[:, g // GPI, j, :], ident[:])
                m.then_inc(pt_ready, 1)

            pe.wait_ge(ld_w, 16 * 12)
            for ho in range(DH):
                for he in range(DH):
                    m = pe.transpose(ps[:, 4, he * D + ho * P:he * D + (ho + 1) * P],
                                     wo_sb[:, ho, he * P:(he + 1) * P], ident[:])
            m.then_inc(su_pe, 1)
            for h in range(DH):
                m = pe.transpose(ps[0:PD, 5, h * P:(h + 1) * P], wt_sb[:, h, :], ident[:])
            m.then_inc(su_pe, 1)
            for hd in range(DH):
                for he in range(DH):
                    m = pe.matmul(ps[:, 6, hd * D:(hd + 1) * D], wq_sb[:, he, hd * P:(hd + 1) * P], wk_sb[:, he, :],
                                  start=(he == 0), stop=(he == DH - 1))
            m.then_inc(su_pe, 1)
            pe.wait_ge(su_wot, 1)
            for hd in range(DH):
                for he in range(DH):
                    m = pe.matmul(ps[:, 7, hd * D:(hd + 1) * D], wv_sb[:, he, hd * P:(hd + 1) * P], woT[:, he, :],
                                  start=(he == 0), stop=(he == DH - 1))
            m.then_inc(su_pe, 1)
            pe.wait_ge(su_wtt, 1)
            for hd in range(DH):
                d = slice(hd * P, (hd + 1) * P)
                pe.matmul(ps[:, 5, hd * 4:hd * 4 + 1], wq_sb[:, 0, d], ident[:, 0:1], start=True, stop=True)
                pe.matmul(ps[:, 5, hd * 4 + 1:hd * 4 + 2], wk_sb[:, 0, d], ident[:, 0:1], start=True, stop=True)
                for he in range(DH):
                    pe.matmul(ps[:, 5, hd * 4 + 2:hd * 4 + 3], wq_sb[:, he, d], bcol[:, 1, he:he + 1],
                              start=(he == 0), stop=(he == DH - 1))
                for he in range(DH):
                    m = pe.matmul(ps[:, 5, 16 + hd:17 + hd], wk_sb[:, he, d], bcol[:, 0, he:he + 1],
                                  start=(he == 0), stop=(he == DH - 1))
            m.then_inc(su_pe, 1)
            pe.wait_ge(su_bbc, 1)
            for he in range(DH):
                pe.matmul(ps[:, 4, 0:D], bbc[:, 1, he, :], woT[:, he, :], start=(he == 0), stop=(he == DH - 1))
            for he in range(DH):
                m = pe.matmul(ps[:, 4, D:D + 1], bbc[:, 0, he, :], bcol[:, 1, he:he + 1],
                              start=(he == 0), stop=(he == DH - 1))
            m.then_inc(su_pe, 1)
            pe.wait_ge(su_done, 1)

            def three(dst, lhs, rhs):
                n = 0
                for h in range(DH):
                    for a, r in ((0, 0), (0, 1), (1, 0)):
                        m = pe.matmul(dst, lhs[a][h], rhs[r][h], start=(n == 0), stop=(n == 3 * DH - 1))
                        n += 1
                return m

            def embed(c, j, bank):
                m = pe.matmul(ps[:, bank, 0:D], pst[:, j * P:(j + 1) * P], wtT[:], start=True, stop=True)
                m.then_inc(h_ready, 1)

            def turn_xn(b, c, j, bank):
                r = nrows(c, j)
                pe.wait_ge(xn_ready, b * NT + c * TC + j + 1)
                for h in range(DH):
                    m = pe.transpose(ps[:, bank, h * P:h * P + r], xn[0:r, j, h * P:(h + 1) * P], ident[0:r, 0:r])
                m.then_inc(xt_ready, 1)

            def values(b, c, j, bank):
                r = nrows(c, j)
                pe.wait_ge(xt_lo, b * NT + c * TC + j + 1)
                s = slice(j * P, j * P + r)
                three(ps[0:r, bank, 0:VW], [[X[:, h, s] for h in range(DH)] for X in (xs_hi, xs_lo)],
                      [[W[:, h, :] for h in range(DH)] for W in (WV_hi, WV_lo)]).then_inc(v_ready, 1)

            def queries(b, c):
                w = width(c) + width(c) % 2
                pe.wait_ge(xt_copied, 2 * (b * NC + c + 1))
                for hd, bank in ((0, T2), (1, AUX)):
                    three(ps[:, bank, 0:w], [[A[:, h, hd * P:(hd + 1) * P] for h in range(DH)] for A in (A_hi, A_lo)],
                          [[xT_at(X, b, h, c * CW, w) for h in range(DH)] for X in (xT_hi, xT_lo)]).then_inc(g_ready, 1)

            def scores_of(b, c, j):
                r = nrows(c, j)
                pe.wait_ge(g_lo, DH * (b * NC + c + 1))
                if c == 0 and j == 0:
                    pe.wait_ge(xt_copied, 2 * NC * (b + 1))
                s = slice(j * P, j * P + r)
                for n in range(3):
                    m = three(ps[0:r, n, 0:SW + 1], [[G[:, h, s] for h in range(DH)] for G in (G_hi, G_lo)],
                              [[xT_at(X, b, h, n * SW, SW + 1) for h in range(DH)] for X in (xT_hi, xT_lo)])
                m.then_inc(s_ready, 1)

            def turn_probs(b, c, j, before):
                t = b * NT + c * TC + j
                r = nrows(c, j)
                pe.wait_ge(exp_done, t + 1)
                for u in range(NC):
                    for s, v in before[u]:
                        pe.wait_ge(s, v)
                    for k in range(TC):
                        kt = u * TC + k
                        m = pe.transpose(ps[:, TB[u], k * P:k * P + r], probs[0:r, kt * P:(kt + 1) * P], ident[0:r, 0:r])
                    m.then_inc(t_ready, 1)

            def attend(b, c, j):
                t = b * NT + c * TC + j
                r = nrows(c, j)
                if c == 0 and j == 0:
                    pe.wait_ge(v_lo, NT * (b + 1))
                n = 0
                for u in range(NC):
                    pe.wait_ge(t_lo, NC * t + u + 1)
                    for kt in range(u * TC, (u + 1) * TC):
                        kr = LASTR if kt == NT - 1 else P
                        for PT, V in ((PT_hi, V_hi), (PT_hi, V_lo), (PT_lo, V_hi)):
                            m = pe.matmul(ps[0:r, OB, 0:D], PT[0:kr, kt, 0:r], v_at(V, b, kt, kr),
                                          start=(n == 0), stop=(n == 3 * NT - 1))
                            n += 1
                m.then_inc(o_ready, 1)

            for c in range(NC):
                pe.wait_ge(pst_ready, c + 1)
                if c:
                    pe.wait_ge(v_f, c * TC)
                for j, bank in ((0, AUX), (1, T0), (2, T1)):
                    if c * TC + j < NIT:
                        embed(c, j, bank)
                for j, bank in ((0, AUX), (1, T0), (2, T1)):
                    turn_xn(0, c, j, bank)
                for j, bank in ((0, T2), (1, AUX), (2, T0)):
                    if j:
                        pe.wait_ge(xt_lo, c * TC + j)
                    values(0, c, j, bank)
            pe.wait_ge(v_f, NT)
            queries(0, 0)
            scores_of(0, 0, 0)

            def body(b, c, has_next):
                t = b * NT + c * TC
                more = has_next or c < NC - 1
                pn = (b + 1) * NT + c * TC if has_next else NB * NT
                hn = (b + 1) * NIT + c * TC
                m = b * NC + c
                bn, cn = nxt(b, c)

                turn_probs(b, c, 0, [[(v_f, pn - 1)], [(v_f, pn)], []])
                scores_of(b, c, 1)
                if has_next:
                    pe.wait_ge(pst_ready, (b + 1) * NC + c + 1)
                    embed(c, 0, AUX)
                    pe.wait_ge(t_lo, NC * t + 1)
                    embed(c, 1, T0)
                    if c < NC - 1:
                        pe.wait_ge(t_lo, NC * t + 2)
                        embed(c, 2, T1)
                attend(b, c, 0)
                if has_next:
                    turn_xn(b + 1, c, 0, AUX)

                nh = min(TC, NIT - c * TC)
                turn_probs(b, c, 1, [[(h_done, hn + 2)], [(h_done, hn + nh)], []] if has_next else [[], [], []])
                scores_of(b, c, 2)
                if has_next:
                    pe.wait_ge(t_lo, NC * (t + 1) + 1)
                    turn_xn(b + 1, c, 1, T0)
                    pe.wait_ge(t_lo, NC * (t + 1) + 2)
                    turn_xn(b + 1, c, 2, T1)
                    pe.wait_ge(xt_lo, pn + 1)
                if more:
                    pe.wait_ge(t_lo, NC * (t + 1) + 3)
                    queries(bn, cn)
                attend(b, c, 1)
                if has_next:
                    pe.wait_ge(g_lo, DH * (m + 2))
                    values(b + 1, c, 0, AUX)

                turn_probs(b, c, 2, [[(xt_lo, pn + 2)], [(xt_lo, pn + 3)], [(g_lo, DH * (m + 1) + 1)]]
                           if has_next else [[], [], [(g_lo, DH * (m + 1) + 1)] if more else []])
                if more:
                    scores_of(bn, cn, 0)
                if has_next:
                    pe.wait_ge(t_lo, NC * (t + 2) + 1)
                    values(b + 1, c, 1, T0)
                    pe.wait_ge(t_lo, NC * (t + 2) + 2)
                    values(b + 1, c, 2, T1)
                attend(b, c, 2)

            batches(pe, body)

            pe.wait_ge(acc_done, NB * NT)
            for h in range(DH):
                for b in range(NB):
                    m = pe.matmul(ps[:, 0, h * NB + b:h * NB + b + 1], acc[:, b, h * P:(h + 1) * P], ones[:, 0:1],
                                  start=True, stop=True)
            m.then_inc(r_pe, 1)
            pe.wait_ge(r_v, 1)
            for h in range(DH):
                m = pe.matmul(ps[0:NB, 1, 0:NE], meanT[:, h, :], wr_sb[:, h, :], start=(h == 0), stop=(h == DH - 1))
            m.then_inc(r_pe, 1)
            pe.wait_ge(r_v, 6)
            pe.matmul(ps[0:NB, 2, 0:NE], ones[0:NB, 0:NB], small[:, 2, :], start=True, stop=True).then_inc(r_pe, 1)
            pe.wait_ge(r_v, 21)
            pe.matmul(ps[:, 3, 0:NB * TOPK], ones[0:NB, :], diag_w[:].rearrange("p b k -> p (b k)"),
                      start=True, stop=True).then_inc(r_pe, 1)

            def turn_x2(b, c, h):
                m = b * NC + c
                pe.wait_ge(x2s_ready, TC * (m + 1))
                for j in range(TC):
                    r = nrows(c, j)
                    i = pe.transpose(ps[:, XB, j * P:j * P + r], x2s[0:r, j, h * P:(h + 1) * P], ident[0:r, 0:r])
                i.then_inc(xf_ready, 1)

            turn_x2(0, 0, 0)
            pe.wait_ge(xf_lod, 1)
            turn_x2(0, 0, 1)

            def ffn(b, c, has_next):
                m = b * NC + c
                n = NF * m
                t = b * NT + c * TC
                w = width(c) + width(c) % 2
                more = has_next or c < NC - 1
                pe.wait_ge(xf_lod, DH * (m + 1))
                if c == 0:
                    pe.wait_ge(w1_lod, b + 1)
                for f in range(NF):
                    k, q = f // FQ, f % FQ
                    if f >= 4:
                        pe.wait_ge(gelu_done, n + f - 3)
                    three(ps[:, f % 4, 0:w],
                          [[W[:, k, h, q * P:(q + 1) * P] for h in range(DH)] for W in (w1_hi, w1_lo)],
                          [[X[:, h, 0:w] for h in range(DH)] for X in (xf_hi, xf_lo)]).then_inc(f_ready, 1)
                if more:
                    turn_x2(*nxt(b, c), 0)
                if c == 0:
                    pe.wait_ge(w2_lod, b + 1)
                for j in range(TC):
                    r = nrows(c, j)
                    pe.wait_ge(y_done, t + j + 1)
                    i = 0
                    for f in range(NF):
                        if j == 0:
                            pe.wait_ge(h_lod, 4 + n + f + 1)
                        k, q = f // FQ, f % FQ
                        for H, W in ((h_hi, w2_hi), (h_hi, w2_lo), (h_lo, w2_hi)):
                            ins = pe.matmul(ps[0:r, Y0 + j, 0:D], H[:, f, j * P:j * P + r], W[:, k, q, :],
                                            start=(i == 0), stop=(i == 3 * NF - 1))
                            i += 1
                    ins.then_inc(y_ready, 1)
                    if j == 0 and more:
                        pe.wait_ge(xf_lod, DH * (m + 1) + 1)
                        turn_x2(*nxt(b, c), 1)

            batches(pe, ffn)


_INS = ["x", "txt"] + ["L0_tok_W", "L0_tok_b", "L0_tok_pos"] + \
    ["L0_attn_" + n for n in ("Wq", "bq", "Wk", "bk", "Wv", "bv", "Wo", "bo")] + \
    ["L0_ffn_" + n for n in ("Wr", "br", "W1", "b1", "W2", "b2", "gamma", "beta")]


def kernel(**inputs):
    import numpy as np
    import concourse.bacc as bacc
    from concourse import mybir as mb
    from concourse.bass_utils import run_bass_kernel_spmd as run

    nc = bacc.Bacc("TRN2", target_bir_lowering=False, num_devices=1)
    arrays, args = {}, []
    for name in _INS:
        a = np.ascontiguousarray(inputs[name])
        arrays[f"in_{name}"] = a
        args.append(nc.dram_tensor(f"in_{name}", a.shape, mb.dt.from_np(a.dtype), kind="ExternalInput").ap())
    args.append(nc.dram_tensor("out_0", (NB, S, D), F32, kind="ExternalOutput").ap())
    build(nc, *args)
    return run(nc, [arrays], core_ids=[0]).results[0]["out_0"]
```

```python
from contextlib import ExitStack

import concourse.bass as bass
from concourse import mybir

F32 = mybir.dt.float32
F32R = mybir.dt.float32r
U32 = mybir.dt.uint32
I32 = mybir.dt.int32
ALU = mybir.AluOpType
ACT = mybir.ActivationFunctionType
AX_X = mybir.AxisListType.X
AX_XY = mybir.AxisListType.XY

P = 128
NB = 8
IMG, PATCH = 224, 7
SIDE = IMG // PATCH
NIMG = SIDE * SIDE
PD = PATCH * PATCH
NTXT = 77
S = NIMG + NTXT
D = 256
DH = D // P
NE, F = 8, 512
FQ = F // P
TOPK = 2
NT = (S + P - 1) // P
TC = 3
NC = NT // TC
CW = TC * P
LASTR = S - (NT - 1) * P
LASTW = S - (NC - 1) * CW
SW = S // 3
SE = S + S % 2
VW = D + 4
EPS = 1e-5
SCALE = 1.0 / float(D) ** 0.5
assert SW * 3 == S and SW % 2 and 3 * SW + 1 <= SE
CAPACITY = float(-(-(NB * S * 5 // 4 + (1 if NB * S * 5 % 4 else 0)) // NE))
NIT = NIMG // P
NF = TOPK * FQ
NHA = 3
NPG = 2 * SIDE // 4
GPI = SIDE // 4


def build(nc, x, txt, Wt, bt, pos, Wq, bq, Wk, bk, Wv, bv, Wo, bo, Wr, br, W1, b1, W2, b2, gamma, beta, out):
    with ExitStack() as ctx:
        def sb(name, shape, dt=F32, into=ctx):
            return into.enter_context(nc.sbuf_tensor(name, shape, dt))

        def sem(name):
            return ctx.enter_context(nc.semaphore(name))

        Z = sb("Z", [P, NB * NT, D])
        ident = sb("ident", [P, P])
        ones = sb("ones", [P, P])
        half_neg = sb("half_neg", [P, TC])
        rstd2 = sb("rstd2", [P, NB * NT])
        nmr2 = sb("nmr2", [P, NB * NT])
        bo_row = sb("bo_row", [P, D])
        acc = sb("acc", [P, NB, D])
        wr_sb = sb("wr_sb", [P, DH, NE])
        br_row = sb("br_row", [NB, NE])
        route_w = sb("route_w", [P, NB * TOPK])
        route_i = sb("route_i", [1, NB * TOPK], I32)

        ph = ExitStack()
        xT_hi = sb("xT_hi", [P, 2, DH, SE], F32R, ph)
        xT_lo = sb("xT_lo", [P, 2, DH, SE], F32R, ph)
        xs_hi = sb("xs_hi", [P, DH, CW], F32R, ph)
        xs_lo = sb("xs_lo", [P, DH, CW], F32R, ph)
        wl = ExitStack()
        img = sb("img", [P, 2, PATCH * IMG], F32, wl)
        imp = sb("imp", [P, 2, SIDE, PD], F32, wl)
        wq_sb = sb("wq_sb", [P, DH, D], F32, wl)
        wk_sb = sb("wk_sb", [P, DH, D], F32, wl)
        wv_sb = sb("wv_sb", [P, DH, D], F32, wl)
        wo_sb = sb("wo_sb", [P, DH, D], F32, wl)
        woT = sb("woT", [P, DH, D], F32, wl)
        fold = sb("fold", [P, DH, VW], F32, wl)
        bcol = sb("bcol", [P, 3, DH], F32, wl)
        bbc = sb("bbc", [P, 2, DH, P], F32, wl)
        wt_sb = sb("wt_sb", [P, DH, PD], F32, wl)
        bt_row = sb("bt_row", [P, D], F32, wl)
        wl.close()
        V_hi = sb("V_hi", [P, 2 * NT, D], F32R, ph)
        V_lo = sb("V_lo", [P, 2 * NT, D], F32R, ph)
        PT_hi = sb("PT_hi", [P, NT, P], F32R, ph)
        PT_lo = sb("PT_lo", [P, NT, P], F32R, ph)
        G_hi = sb("G_hi", [P, DH, CW], F32R, ph)
        G_lo = sb("G_lo", [P, DH, CW], F32R, ph)
        A_hi = sb("A_hi", [P, DH, D], F32R, ph)
        A_lo = sb("A_lo", [P, DH, D], F32R, ph)
        WV_hi = sb("WV_hi", [P, DH, VW], F32R, ph)
        WV_lo = sb("WV_lo", [P, DH, VW], F32R, ph)
        probs = sb("probs", [P, NT * P], F32, ph)
        xn = sb("xn", [P, TC, D], F32, ph)
        vf = sb("vf", [P, 2, VW], F32, ph)
        v_bias = sb("v_bias", [P, VW], F32, ph)
        g_bias = sb("g_bias", [P, DH], F32, ph)
        posb = sb("posb", [P, NIT, D], F32, ph)
        wtT = sb("wtT", [PD, D], F32, ph)
        pst = sb("pst", [PD, CW], F32, ph)
        st1 = sb("st1", [P, TC, 6], F32, ph)
        mv1 = sb("mv1", [P, TC, 2], F32, ph)
        ve1 = sb("ve1", [P, TC], F32, ph)
        rs1 = sb("rs1", [P, TC], F32, ph)
        st2 = sb("st2", [P, TC, 6], F32, ph)
        mv2 = sb("mv2", [P, TC, 2], F32, ph)
        ve2 = sb("ve2", [P, TC], F32, ph)
        rs2 = sb("rs2", [P, TC], F32, ph)
        nm2 = sb("nm2", [P, TC], F32, ph)
        zs = sb("zs", [P, 2, D], F32, ph)
        x2t = sb("x2t", [P, D], F32, ph)
        smax = sb("smax", [P, TC, 6], F32, ph)
        mask = sb("mask", [P, NB * NT], F32, ph)
        q_zero = sb("q_zero", [P, 2], F32, ph)
        c_row = sb("c_row", [P, NB * NT], F32, ph)
        ph.close()

        ff = ExitStack()
        x2s = sb("x2s", [P, TC, D], F32, ff)
        xf_hi = sb("xf_hi", [P, DH, CW], F32R, ff)
        xf_lo = sb("xf_lo", [P, DH, CW], F32R, ff)
        small = sb("small", [NB, 16, NE], F32, ff)
        top_i = sb("top_i", [NB, NE], U32, ff)
        diag_w = sb("diag_w", [NB, NB, TOPK], F32, ff)
        meanT = sb("meanT", [P, DH, NB], F32, ff)
        gamma_row = sb("gamma_row", [P, D], F32, ff)
        beta_row = sb("beta_row", [P, D], F32, ff)
        h_hi = sb("h_hi", [P, TOPK * FQ, CW], F32R, ff)
        h_lo = sb("h_lo", [P, TOPK * FQ, CW], F32R, ff)
        w1_hi = sb("w1_hi", [P, TOPK, DH, F], F32R, ff)
        w1_lo = sb("w1_lo", [P, TOPK, DH, F], F32R, ff)
        w2_hi = sb("w2_hi", [P, 2 * TOPK, FQ, D], F32R, ff)
        w2_lo = sb("w2_lo", [P, 2 * TOPK, FQ, D], F32R, ff)
        w1_raw = sb("w1_raw", [P, TOPK, DH, F], F32, ff)
        w2_raw = sb("w2_raw", [P, TOPK, FQ, D], F32, ff)
        b2_raw = sb("b2_raw", [P, TOPK, D], F32, ff)
        b1_sb = sb("b1_sb", [P, NB * TOPK * FQ], F32, ff)
        b1_cur = sb("b1_cur", [P, NF], F32, ff)
        w_cur = sb("w_cur", [P, TOPK], F32, ff)
        b2_sum = sb("b2_sum", [P, D], F32, ff)
        gel = sb("gel", [P, 4, CW], F32, ff)
        x2b = sb("x2b", [P, TC, D], F32, ff)
        yb = sb("yb", [P, TC, D], F32, ff)
        ob = sb("ob", [P, TC, D], F32, ff)
        st3 = sb("st3", [P, TC, 6], F32, ff)
        mv3 = sb("mv3", [P, TC, 2], F32, ff)
        ve3 = sb("ve3", [P, TC], F32, ff)
        rs3 = sb("rs3", [P, TC], F32, ff)
        ff.close()

        ps = ctx.enter_context(nc.psum_tensor("ps", [P, 8, 512], F32))
        scores = ps[:, 0:3, 0:SW]
        T0, T1, T2, AUX, OB = 3, 4, 5, 6, 7
        TB = (T0, T1, T2)
        SB = (0, 1, 2)

        def embed_psum(T):
            return ps[:, T % 8, 0:D]

        ld_w = sem("ld_w")
        ld_img = [sem(f"ld_img{g}") for g in range(2)]
        posb_done = sem("posb_done")
        ld_txt = sem("ld_txt")
        ld_rows = sem("ld_rows")
        ld_ffn = sem("ld_ffn")
        c_ident = sem("c_ident")
        c_zero = sem("c_zero")
        su_pe = sem("su_pe")
        su_v = sem("su_v")
        su_wot = sem("su_wot")
        su_wtt = sem("su_wtt")
        su_bbc = sem("su_bbc")
        su_done = sem("su_done")
        im_dve = sem("im_dve")
        im_act = sem("im_act")
        pt_ready = sem("pt_ready")
        pt_even = sem("pt_even")
        pt_odd = sem("pt_odd")
        pst_ready = sem("pst_ready")
        h_ready = sem("h_ready")
        h_done = sem("h_done")
        st1_done = sem("st1_done")
        mv1_done = sem("mv1_done")
        ve1_done = sem("ve1_done")
        rs1_done = sem("rs1_done")
        xn_ready = sem("xn_ready")
        zb_ready = sem("zb_ready")
        xt_ready = sem("xt_ready")
        xt_hi = sem("xt_hi")
        xt_lo = sem("xt_lo")
        xt_copied = sem("xt_copied")
        v_ready = sem("v_ready")
        v_f = sem("v_f")
        v_hi = sem("v_hi")
        v_lo = sem("v_lo")
        v_info = sem("v_info")
        g_ready = sem("g_ready")
        g_hi = sem("g_hi")
        g_lo = sem("g_lo")
        s_ready = sem("s_ready")
        max_done = sem("max_done")
        full_max = sem("full_max")
        shift_done = sem("shift_done")
        exp_done = sem("exp_done")
        t_ready = sem("t_ready")
        t_hi = sem("t_hi")
        t_lo = sem("t_lo")
        o_ready = sem("o_ready")
        rinv_done = sem("rinv_done")
        rs_done = sem("rs_done")
        o_done = sem("o_done")
        st2_done = sem("st2_done")
        mv2_done = sem("mv2_done")
        ve2_done = sem("ve2_done")
        rs2_done = sem("rs2_done")
        nmr2_done = sem("nmr2_done")
        x2_done = sem("x2_done")
        acc_done = sem("acc_done")
        r_pe = sem("r_pe")
        r_v = sem("r_v")
        r_a = sem("r_a")
        r_idx = sem("r_idx")
        w1_in = [sem(f"w1_in{k}") for k in range(TOPK)]
        w2_in = sem("w2_in")
        b1_in = sem("b1_in")
        b2_in = sem("b2_in")
        w1_hid = sem("w1_hid")
        w1_lod = sem("w1_lod")
        w2_hid = sem("w2_hid")
        w2_lod = sem("w2_lod")
        cur_b1 = sem("cur_b1")
        cur_w = sem("cur_w")
        b2_half = sem("b2_half")
        b2_done = sem("b2_done")
        z_back = sem("z_back")
        kept2 = sem("kept2")
        x2s_ready = sem("x2s_ready")
        zbeta = sem("zbeta")
        x2b_ready = sem("x2b_ready")
        xf_ready = sem("xf_ready")
        xf_hid = sem("xf_hid")
        xf_lod = sem("xf_lod")
        f_ready = sem("f_ready")
        gelu_done = sem("gelu_done")
        h_hid = sem("h_hid")
        h_hid_act = sem("h_hid_act")
        h_lod = sem("h_lod")
        y_ready = sem("y_ready")
        y_done = sem("y_done")
        st3_done = sem("st3_done")
        mv3_done = sem("mv3_done")
        ve3_done = sem("ve3_done")
        rs3_done = sem("rs3_done")
        nrm_done = sem("nrm_done")
        gam_done = sem("gam_done")
        out_ready = sem("out_ready")
        stored = [sem(f"stored{j}") for j in range(TC)]

        XB, Y0 = 4, 5

        def batches(eng, body):
            with eng.Fori(0, NB - 1) as b:
                for c in range(NC):
                    body(b, c, True)
            for c in range(NC):
                body(NB - 1, c, False)

        def width(c):
            return LASTW if c == NC - 1 else CW

        def nrows(c, j):
            return LASTR if c == NC - 1 and j == TC - 1 else P

        def nxt(b, c):
            return (b + 1, 0) if c == NC - 1 else (b, c + 1)

        def wait_apart(eng, counter, value):
            eng.wait_ge(counter, value)
            eng.sem_inc(waits_apart, 1)

        def z_at(t, r):
            return Z[0:r, bass.ds(t, 1), :].rearrange("p o d -> p (o d)")

        def v_at(V, b, t, r):
            return V[0:r, bass.ds((b % 2) * NT + t, 1), :].rearrange("p o d -> p (o d)")

        def patches(b, lo=0, n=NIMG):
            first = b * NT + NIT // 2
            return Z[0:PD, bass.ds(first, NIT // 2), :].rearrange("p t d -> p (t d)")[:, lo:lo + n]

        def w2_at(W, b, k):
            return W[:, bass.ds((b % 2) * TOPK + k, 1), :, :].rearrange("p o q d -> p (o q d)")

        def xT_at(X, b, h, lo, n):
            return X[:, bass.ds(b % 2, 1), h, lo:lo + n].rearrange("p o n -> p (o n)")

        def xt_psum(bank, r):
            return ps[:, bank, 0:DH * P].rearrange("p (h t) -> p h t", h=DH)[:, :, 0:r]

        def image_views(g):
            return (imp[:, g].rearrange("p j (r k) -> p j r k", r=PATCH),
                    img[:, g, :].rearrange("p (r j k) -> p j r k", r=PATCH, j=SIDE))

        def patch_views(g):
            src = ps[0:PD, g % 4, :].rearrange("p (j b i) -> p b i j", j=4, b=NB // 2)
            b0 = (g // GPI) * 4
            return [(patches(b0 + b).rearrange("p (i j) -> p i j", j=SIDE)[:, :, (g % GPI) * 4:(g % GPI) * 4 + 4],
                     src[:, b]) for b in range(4)]

        waits_apart = sem("waits_apart")

        block = ctx.enter_context(nc.Block())

        @block.sync
        def _(sp):
            for g in range(2):
                sp.dma_start(img[:, g, :], x[4 * g:4 * g + 4, 0].rearrange("b (i r) w -> (b i) (r w)", r=PATCH)
                             ).then_inc(ld_img[g], 16)
            for w_dram, w_sb in ((Wq, wq_sb), (Wk, wk_sb), (Wv, wv_sb), (Wo, wo_sb)):
                sp.dma_start(w_sb[:], w_dram.rearrange("(h p) d -> p h d", p=P)).then_inc(ld_w, 16)
            sp.dma_start(wt_sb[:], Wt.rearrange("(h p) k -> p h k", p=P)).then_inc(ld_w, 16)
            with nc.allow_non_contiguous_dma("three bias vectors laid on partitions, once"):
                for n, b_dram in enumerate((bq, bk, bv)):
                    sp.dma_start(bcol[:, n, :], b_dram.rearrange("(h p) -> p h", p=P)).then_inc(ld_w, 16)
            sp.dma_start(bt_row[:], bt.partition_broadcast(P)).then_inc(ld_w, 16)
            sp.dma_start(v_bias[:, D:D + 1], bq[0:1].partition_broadcast(P)).then_inc(ld_w, 16)
            sp.dma_start(v_bias[:, D + 1:D + 2], bk[0:1].partition_broadcast(P)).then_inc(ld_w, 16)
            sp.dma_start(posb[:], pos[0].rearrange("(t p) d -> p t d", p=P)).then_inc(ld_w, 16)
            sp.dma_start(Z[0:NTXT, :, :].rearrange("p (b t) d -> p b t d", t=NT)[:, :, NT - 1, :],
                         txt.rearrange("b p d -> p b d")).then_inc(ld_txt, 16)
            sp.dma_start(bo_row[:], bo.partition_broadcast(P)).then_inc(ld_rows, 16)
            sp.dma_start(br_row[:], br.partition_broadcast(NB)).then_inc(ld_rows, 16)
            sp.dma_start(wr_sb[:], Wr.rearrange("(h p) e -> p h e", p=P)).then_inc(ld_rows, 16)

            sp.wait_ge(x2s_ready, TC)
            sp.dma_start(gamma_row[:], gamma.partition_broadcast(P)).then_inc(ld_ffn, 16)
            sp.dma_start(beta_row[:], beta.partition_broadcast(P)).then_inc(ld_ffn, 16)
            sp.wait_ge(r_v, 16)
            sp.dma_start(route_i[:], top_i[:, 0:TOPK].bitcast(I32)).then_inc(r_idx, 16)
            sp.wait_ge(r_idx, 16)

            def load_experts(b):
                experts = [sp.value_load(route_i[0:1, bass.ds(b * TOPK + k, 1)], min_val=0, max_val=NE - 1)
                           for k in range(TOPK)]
                for k, e in enumerate(experts):
                    sp.dma_start(w1_raw[:, k], W1[bass.ds(e, 1)].rearrange("o (h p) f -> p (o h) f", p=P)
                                 ).then_inc(w1_in[k], 16)
                for k, e in enumerate(experts):
                    with nc.allow_non_contiguous_dma("an expert's bias laid on partitions"):
                        sp.dma_start(b1_sb[:, bass.ds((b * TOPK + k) * FQ, FQ)],
                                     b1[bass.ds(e, 1)].rearrange("o (q p) -> p (o q)", p=P)).then_inc(b1_in, 16)
                    sp.dma_start(b2_raw[:, k], b2[bass.ds(e, 1)].rearrange("o d -> (o d)").partition_broadcast(P)
                                 ).then_inc(b2_in, 16)
                for k, e in enumerate(experts):
                    sp.dma_start(w2_raw[:, k], W2[bass.ds(e, 1)].rearrange("o (q p) d -> p (o q) d", p=P)
                                 ).then_inc(w2_in, 16)

            load_experts(0)

            def store(b, c, has_next):
                if c == 0 and has_next:
                    sp.wait_ge(w1_lod, TOPK * (b + 1))
                    sp.wait_ge(w2_lod, TOPK * (b + 1))
                    sp.wait_ge(b2_done, b + 1)
                    load_experts(b + 1)
                for j in range(TC):
                    r = nrows(c, j)
                    sp.wait_ge(out_ready, TC + b * NT + c * TC + j + 1)
                    sp.dma_start(out[bass.ds(b, 1), c * CW + j * P:c * CW + j * P + r, :].rearrange("o p d -> (o p) d"),
                                 ob[0:r, j, :]).then_inc(stored[j], 16)

            batches(sp, store)
            for j in range(TC):
                sp.wait_ge(stored[j], 16 * (1 + NB * NC))

        @block.gpsimd
        def _(pool):
            pool.memset(ones[:], 1.0).then_inc(c_zero, 1)
            pool.memset(half_neg[:], -0.5).then_inc(c_zero, 1)
            pool.memset(probs[:, S:], 0.0).then_inc(c_zero, 1)
            pool.memset(mv1[:], 0.0).then_inc(c_zero, 1)
            pool.memset(x2t[:], 0.0).then_inc(x2_done, 2)
            pool.memset(acc[:], 0.0).then_inc(c_zero, 1)
            for X in (xT_hi, xT_lo):
                for par in range(2):
                    pool.memset(X[:, par, :, S:SE].bitcast(F32), 0.0).then_inc(c_zero, 1)
            pool.wait_ge(c_zero, 1)
            pool.affine_select(out=ident[:], in_=ones[:], compare_op=ALU.is_equal, fill=0.0, base=0,
                               pattern=[[-1, P]], channel_multiplier=1).then_inc(c_ident, 1)

            pool.wait_ge(ld_w, 16 * 12)
            for n, which in enumerate((0, 2)):
                for h in range(DH):
                    pool.tensor_scalar(bbc[:, n, h, :], ones[:], bcol[:, which, h:h + 1], None, ALU.mult
                                       ).then_inc(su_bbc, 1)
            pool.memset(fold[:], 0.0).then_inc(su_bbc, 1)
            pool.tensor_tensor(posb[:], posb[:], bt_row[:].unsqueeze(1).to_broadcast([P, NIT, D]), ALU.add
                               ).then_inc(posb_done, 1)

            def ln1_and_bo(b, c):
                t = b * NT + c * TC
                wait_apart(pool, mv1_done, t + TC)
                pool.tensor_scalar(ve1[:], mv1[:, :, 1], EPS, None, ALU.add).then_inc(ve1_done, 1)
                pool.wait_ge(ve1_done, b * NC + c + 1)
                pool.tensor_tensor(rs1[:], ve1[:], half_neg[:], ALU.pow).then_inc(rs1_done, 1)
                for j in range(TC):
                    r = nrows(c, j)
                    wait_apart(pool, xn_ready, t + j + 1)
                    pool.tensor_tensor(z_at(t + j, r), z_at(t + j, r), bo_row[0:r, :], ALU.add).then_inc(zb_ready, 1)

            def ln2_sum(b, c, j):
                r = nrows(c, j)
                t = b * NT + c * TC + j
                k = (c * TC + j) % 2
                wait_apart(pool, mv2_done, t + 1)
                pool.tensor_scalar(ve2[0:r, j:j + 1], mv2[0:r, j, 1:2], EPS, None, ALU.add).then_inc(ve2_done, 1)
                pool.wait_ge(ve2_done, t + 1)
                pool.tensor_tensor(rs2[0:r, j:j + 1], ve2[0:r, j:j + 1], half_neg[0:r, 0:1], ALU.pow
                                   ).then_inc(rs2_done, 1)
                wait_apart(pool, rs2_done, t + 1)
                pool.tensor_scalar(nm2[0:r, j:j + 1], mv2[0:r, j, 0:1], rs2[0:r, j:j + 1], -1.0,
                                   ALU.mult, ALU.mult).then_inc(nmr2_done, 1)
                pool.tensor_copy(rstd2[0:r, bass.ds(t, 1)], rs2[0:r, j:j + 1]).then_inc(kept2, 1)
                wait_apart(pool, nmr2_done, t + 1)
                pool.tensor_copy(nmr2[0:r, bass.ds(t, 1)], nm2[0:r, j:j + 1]).then_inc(kept2, 1)
                pool.tensor_scalar(x2t[0:r, :], zs[0:r, k, :], rs2[0:r, j:j + 1], nm2[0:r, j:j + 1],
                                   ALU.mult, ALU.add).then_inc(x2_done, 1)
                wait_apart(pool, x2_done, 2 + t + 1)
                a = acc[0:r, bass.ds(b, 1), :].rearrange("p o d -> p (o d)")
                pool.tensor_tensor(a, a, x2t[0:r, :], ALU.add).then_inc(acc_done, 1)

            pool.wait_ge(c_zero, 9)
            pool.wait_ge(ld_rows, 16 * 3)
            for c in range(NC):
                ln1_and_bo(0, c)

            def body(b, c, has_next):
                if has_next:
                    ln1_and_bo(b + 1, c)
                ln2_sum(b, c, 0)
                ln2_sum(b, c, 1)
                ln2_sum(b, c, 2)

            batches(pool, body)

            def add_beta(b, c):
                t = b * NT + c * TC
                for j in range(TC):
                    r = nrows(c, j)
                    wait_apart(pool, x2s_ready, t + j + 1)
                    pool.tensor_tensor(z_at(t + j, r), z_at(t + j, r), beta_row[0:r, :], ALU.add).then_inc(zbeta, 1)

            def make_x2b(b, c, tiles=range(TC)):
                wait_apart(pool, b2_done, b + 1)
                for j in tiles:
                    r = nrows(c, j)
                    pool.tensor_tensor(x2b[0:r, j, :], x2s[0:r, j, :], b2_sum[0:r, :], ALU.add
                                       ).then_inc(x2b_ready, 1)

            pool.wait_ge(ld_ffn, 32)
            for j in range(TC):
                pool.memset(ve3[:, j:j + 1], 1.0).then_inc(stored[j], 16)
            pool.memset(rs3[:], 0.0).then_inc(out_ready, TC)
            add_beta(0, 0)
            make_x2b(0, 0)

            def ffn(b, c, has_next):
                t = b * NT + c * TC
                more = has_next or c < NC - 1
                if more:
                    add_beta(*nxt(b, c))
                for j in range(TC):
                    r = nrows(c, j)
                    wait_apart(pool, mv3_done, t + j + 1)
                    pool.tensor_scalar(ve3[0:r, j:j + 1], mv3[0:r, j, 1:2], EPS, None, ALU.add).then_inc(ve3_done, 1)
                    pool.wait_ge(ve3_done, t + j + 1)
                    pool.tensor_tensor(rs3[0:r, j:j + 1], ve3[0:r, j:j + 1], half_neg[0:r, 0:1], ALU.pow
                                       ).then_inc(rs3_done, 1)
                    if more:
                        make_x2b(*nxt(b, c), [j])
                for j in range(TC):
                    r = nrows(c, j)
                    pool.wait_ge(gam_done, t + j + 1)
                    wait_apart(pool, stored[j], 16 * (b * NC + c + 1))
                    pool.tensor_tensor(ob[0:r, j, :], yb[0:r, j, :], z_at(t + j, r), ALU.add).then_inc(out_ready, 1)

            batches(pool, ffn)

        @block.scalar
        def _(act):
            act.wait_ge(ld_img[1], 16)
            act.activation(*image_views(1), ACT.Copy).then_inc(im_act, 1)
            for g in range(1, NPG, 2):
                act.wait_ge(pt_ready, g + 1)
                for dst, src in patch_views(g):
                    ins = act.activation(dst, src, ACT.Copy)
                ins.then_inc(pt_odd, 1)

            def stage_patches(b, c):
                n = width(c) - NTXT if c == NC - 1 else CW
                act.activation(pst[:, 0:n], patches(b, c * CW, n), ACT.Copy).then_inc(pst_ready, 1)

            def split_xt(b, c, j, bank):
                r = nrows(c, j)
                act.wait_ge(xt_ready, b * NT + c * TC + j + 1)
                act.activation(xs_hi[:, :, j * P:j * P + r], xt_psum(bank, r), ACT.Copy).then_inc(xt_hi, 1)

            def copy_xT(b, c):
                n = width(c)
                wait_apart(act, xt_hi, b * NT + c * TC + TC)
                act.activation(xT_hi[:, bass.ds(b % 2, 1), :, c * CW:c * CW + n].rearrange("p o h n -> p (o h) n"),
                               xs_hi[:, :, 0:n], ACT.Copy).then_inc(xt_copied, 1)

            def split_v(b, c, j):
                r = nrows(c, j)
                wait_apart(act, v_f, b * NT + c * TC + j + 1)
                act.activation(v_at(V_hi, b, c * TC + j, r), vf[0:r, j % 2, 0:D], ACT.Copy).then_inc(v_hi, 1)

            def split_g(b, c):
                w = width(c)
                for h, bank in ((0, T2), (1, AUX)):
                    act.wait_ge(g_ready, DH * (b * NC + c) + h + 1)
                    act.activation(G_hi[:, h, 0:w], ps[:, bank, 0:w], ACT.Identity, bias=g_bias[:, h:h + 1]
                                   ).then_inc(g_hi, 1)

            def exp_tile(b, c, j):
                r = nrows(c, j)
                act.wait_ge(shift_done, b * NT + c * TC + j + 1)
                act.activation(probs[0:r, 0:S].rearrange("p (a b) -> p a b", b=SW), scores[0:r], ACT.Exp,
                               bias=smax[0:r, j, 2:3], scale=SCALE, accum_out=smax[0:r, j, 3:4]).then_inc(exp_done, 1)

            act.wait_ge(su_done, 1)
            for c in range(NC):
                if c:
                    act.wait_ge(xt_copied, 2 * c)
                for j, bank in enumerate(TB):
                    split_xt(0, c, j, bank)
                copy_xT(0, c)
                for j in range(TC):
                    split_v(0, c, j)
            split_g(0, 0)
            act.wait_ge(c_zero, 9)
            act.wait_ge(pt_even, NPG // 2)
            act.wait_ge(pt_odd, NPG // 2)
            exp_tile(0, 0, 0)

            def body(b, c, has_next):
                t = b * NT + c * TC
                more = has_next or c < NC - 1
                if has_next:
                    wait_apart(act, h_ready, (b + 1) * NIT + c * TC)
                    stage_patches(b + 1, c)
                for j in range(TC):
                    for u in range(NC):
                        act.wait_ge(t_ready, NC * (t + j) + u + 1)
                        act.activation(PT_hi[:, TC * u:TC * (u + 1), :].rearrange("p a b -> p (a b)"),
                                       ps[:, TB[u], 0:CW], ACT.Copy).then_inc(t_hi, 1)
                    if j == 1:
                        if has_next:
                            act.wait_ge(xt_copied, 2 * ((b + 1) * NC + c))
                            split_xt(b + 1, c, 0, AUX)
                            split_xt(b + 1, c, 1, T0)
                            split_xt(b + 1, c, 2, T1)
                        if more:
                            split_g(*nxt(b, c))
                    if j < TC - 1:
                        exp_tile(b, c, j + 1)
                    elif more:
                        exp_tile(*nxt(b, c), 0)
                    if j == 1:
                        if has_next:
                            copy_xT(b + 1, c)
                            split_v(b + 1, c, 0)
                    if j == 2 and has_next:
                        split_v(b + 1, c, 1)
                        split_v(b + 1, c, 2)

            batches(act, body)

            def split_w1(b):
                for k in range(TOPK):
                    act.wait_ge(w1_in[k], 16 * (b + 1))
                    act.activation(w1_hi[:, k].rearrange("p a b -> p (a b)"), w1_raw[:, k].rearrange("p a b -> p (a b)"),
                                   ACT.Copy).then_inc(w1_hid, 1)

            def split_w2(b):
                wait_apart(act, cur_w, b + 1)
                wait_apart(act, w2_in, 16 * TOPK * (b + 1))
                for k in range(TOPK):
                    act.activation(w2_at(w2_hi, b, k), w2_raw[:, k].rearrange("p a b -> p (a b)"),
                                   ACT.Copy, scale=w_cur[:, k:k + 1]).then_inc(w2_hid, 1)

            def split_xf(b, c, h):
                w = width(c)
                act.wait_ge(xf_ready, DH * (b * NC + c) + h + 1)
                act.activation(xf_hi[:, h, 0:w], ps[:, XB, 0:w], ACT.Copy).then_inc(xf_hid, 1)

            split_xf(0, 0, 0)
            split_xf(0, 0, 1)

            for n, (need, dst, src, w) in enumerate(((4, 1, 0, NE), (12, 4, 3, NE), (17, 7, 6, TOPK))):
                act.wait_ge(r_v, need)
                act.activation(small[:, dst, 0:w], small[:, src, 0:w], ACT.Exp, bias=small[:, 9 + n, 0:1],
                               accum_out=small[:, 9 + n, 1:2]).then_inc(r_a, 1)

            split_w1(0)
            split_w2(0)

            def ffn(b, c, has_next):
                n = NF * (b * NC + c)
                w = width(c)
                if c == 0:
                    act.wait_ge(cur_b1, b + 1)
                for f in range(NF):
                    act.wait_ge(f_ready, n + f + 1)
                    act.wait_ge(h_lod, n + f + 1)
                    act.activation(gel[:, f % 4, 0:w], ps[:, f % 4, 0:w], ACT.Gelu,
                                   bias=b1_cur[:, f:f + 1]).then_inc(gelu_done, 1)
                    if f < NHA:
                        act.wait_ge(gelu_done, n + f + 1)
                        act.activation(h_hi[:, f, 0:w], gel[:, f % 4, 0:w], ACT.Copy).then_inc(h_hid_act, 1)
                    if c == 1 and f == 1 and has_next:
                        split_w2(b + 1)
                if has_next or c < NC - 1:
                    split_xf(*nxt(b, c), 0)
                if c == NC - 1 and has_next:
                    split_w1(b + 1)
                if has_next or c < NC - 1:
                    split_xf(*nxt(b, c), 1)

            batches(act, ffn)

        @block.vector
        def _(dve):
            dve.wait_ge(ld_img[0], 16)
            dve.tensor_copy(*image_views(0)).then_inc(im_dve, 1)
            for g in range(0, NPG, 2):
                dve.wait_ge(pt_ready, g + 1)
                for dst, src in patch_views(g):
                    ins = dve.tensor_copy(dst, src)
                ins.then_inc(pt_even, 1)

            step = [0]

            def link(ins):
                step[0] += 1
                ins.then_inc(su_v, 1)
                dve.wait_ge(su_v, step[0])

            dve.wait_ge(ld_w, 16 * 12)
            dve.wait_ge(c_zero, 9)
            dve.wait_ge(su_pe, 1)
            dve.tensor_copy(woT[:].rearrange("p h d -> p (h d)"), ps[:, 4, :]).then_inc(su_wot, 1)
            dve.wait_ge(su_pe, 2)
            dve.tensor_copy(wtT[:], ps[0:PD, 5, 0:D]).then_inc(su_wtt, 1)
            dve.wait_ge(su_pe, 3)
            a2 = "p h d -> p (h d)"
            link(dve.tensor_copy(A_hi[:].rearrange(a2), ps[:, 6, :]))
            link(dve.tensor_tensor(A_lo[:].rearrange(a2), ps[:, 6, :], A_hi[:].rearrange(a2).bitcast(F32), ALU.subtract))
            dve.wait_ge(su_pe, 4)
            dve.wait_ge(su_bbc, 5)
            link(dve.tensor_copy(fold[:, :, 0:D], ps[:, 7, :].rearrange("p (h d) -> p h d", h=DH)))
            dve.wait_ge(su_pe, 5)
            link(dve.tensor_copy(fold[:, :, D:D + 3], ps[:, 5, 0:8].rearrange("p (h d) -> p h d", h=DH)[:, :, 0:3]))
            link(dve.tensor_copy(g_bias[:], ps[:, 5, 16:16 + DH]))
            link(dve.tensor_copy(WV_hi[:], fold[:]))
            link(dve.tensor_tensor(WV_lo[:], fold[:], WV_hi[:].bitcast(F32), ALU.subtract))
            dve.wait_ge(su_pe, 6)
            link(dve.tensor_copy(v_bias[:, 0:D], ps[:, 4, 0:D]))
            link(dve.tensor_copy(v_bias[:, D + 2:D + 3], ps[:, 4, D:D + 1]))
            dve.memset(v_bias[:, D + 3:VW], 0.0).then_inc(su_done, 1)
            dve.wait_ge(su_done, 1)
            dve.wait_ge(posb_done, 1)
            dve.wait_ge(ld_txt, 16)

            def add_tokens(b, c, at):
                t = b * NT + c * TC
                for j in range(TC):
                    T = c * TC + j
                    if T < NIT:
                        dve.wait_ge(h_ready, b * NIT + T + 1)
                        dve.tensor_tensor(z_at(t + j, P), at[j], posb[:, T, :], ALU.add).then_inc(h_done, 1)

            def moments(b, c):
                t = b * NT + c * TC
                for j in range(TC):
                    T = c * TC + j
                    r = nrows(c, j)
                    if T < NIT:
                        wait_apart(dve, h_done, b * NIT + T + 1)
                    dve.bn_stats(st1[0:r, j, :], z_at(t + j, r)).then_inc(st1_done, 1)
                for j in range(TC):
                    r = nrows(c, j)
                    wait_apart(dve, st1_done, t + j + 1)
                    dve.bn_aggr(mv1[0:r, j, :], st1[0:r, j, :]).then_inc(mv1_done, 1)

            def normal1(b, c):
                t = b * NT + c * TC
                dve.wait_ge(rs1_done, b * NC + c + 1)
                for j in range(TC):
                    r = nrows(c, j)
                    dve.tensor_scalar(xn[0:r, j, :], z_at(t + j, r), mv1[0:r, j, 0:1], rs1[0:r, j:j + 1],
                                      ALU.subtract, ALU.mult).then_inc(xn_ready, 1)

            def low_xt(b, c, j, bank):
                r = nrows(c, j)
                s = slice(j * P, j * P + r)
                dve.wait_ge(xt_hi, b * NT + c * TC + j + 1)
                dve.tensor_tensor(xs_lo[:, :, s], xt_psum(bank, r), xs_hi[:, :, s].bitcast(F32), ALU.subtract
                                  ).then_inc(xt_lo, 1)

            def copy_xT(b, c):
                n = width(c)
                dve.wait_ge(xt_lo, b * NT + c * TC + TC)
                dve.tensor_copy(xT_lo[:, bass.ds(b % 2, 1), :, c * CW:c * CW + n].rearrange("p o h n -> p (o h) n"),
                                xs_lo[:, :, 0:n]).then_inc(xt_copied, 1)

            def value_sum(b, c, j, bank):
                r = nrows(c, j)
                t = b * NT + c * TC + j
                used = 3 * (t if j == 0 else t - 1)
                if type(used) is not int or used > 0:
                    dve.wait_ge(v_info, used)
                dve.wait_ge(v_ready, t + 1)
                dve.tensor_tensor(vf[0:r, j % 2, :], ps[0:r, bank, 0:VW], v_bias[0:r, :], ALU.add).then_inc(v_f, 1)

            def low_v(b, c, j):
                t = b * NT + c * TC + j
                r = nrows(c, j)
                dve.wait_ge(v_f, t + 1)
                qz = q_zero[0:r, j % 2:j % 2 + 1]
                dve.tensor_scalar(qz, vf[0:r, j % 2, D:D + 1], 0.0, None, ALU.not_equal).then_inc(v_info, 1)
                dve.tensor_copy(c_row[0:r, bass.ds(t, 1)], vf[0:r, j % 2, D + 2:D + 3]).then_inc(v_info, 1)
                dve.wait_ge(v_hi, t + 1)
                dve.tensor_tensor(v_at(V_lo, b, c * TC + j, r), vf[0:r, j % 2, 0:D], v_at(V_hi, b, c * TC + j, r).bitcast(F32),
                                  ALU.subtract).then_inc(v_lo, 1)
                dve.wait_ge(v_info, 3 * t + 2)
                dve.tensor_scalar(mask[0:r, bass.ds(t, 1)], vf[0:r, j % 2, D + 1:D + 2], 0.0, qz, ALU.not_equal, ALU.mult
                                  ).then_inc(v_info, 1)

            def low_g(b, c):
                w = width(c)
                for h, bank in ((0, T2), (1, AUX)):
                    dve.wait_ge(g_hi, DH * (b * NC + c) + h + 1)
                    dve.scalar_tensor_tensor(out=G_lo[:, h, 0:w], in0=ps[:, bank, 0:w], scalar=g_bias[:, h:h + 1],
                                             in1=G_hi[:, h, 0:w].bitcast(F32), op0=ALU.add, op1=ALU.subtract
                                             ).then_inc(g_lo, 1)

            def shift(b, c, j):
                t = b * NT + c * TC + j
                r = nrows(c, j)
                cr = c_row[0:r, bass.ds(t, 1)]
                dve.wait_ge(v_info, 3 * (t + 1))
                dve.wait_ge(s_ready, t + 1)
                dve.reduce_max(smax[0:r, j, 0:1], scores[0:r], AX_XY).then_inc(max_done, 1)
                dve.wait_ge(max_done, t + 1)
                dve.tensor_tensor(smax[0:r, j, 1:2], smax[0:r, j, 0:1], cr, ALU.add).then_inc(full_max, 1)
                dve.wait_ge(full_max, t + 1)
                dve.tensor_scalar(smax[0:r, j, 2:3], cr, smax[0:r, j, 1:2], SCALE, ALU.subtract, ALU.mult
                                  ).then_inc(shift_done, 1)

            def invert_sum(b, c, j):
                t = b * NT + c * TC + j
                r = nrows(c, j)
                dve.wait_ge(exp_done, t + 1)
                dve.reciprocal(smax[0:r, j, 4:5], smax[0:r, j, 3:4]).then_inc(rinv_done, 1)

            def mask_sum(b, c, j):
                t = b * NT + c * TC + j
                r = nrows(c, j)
                dve.wait_ge(rinv_done, t + 1)
                dve.tensor_tensor(smax[0:r, j, 5:6], mask[0:r, bass.ds(t, 1)], smax[0:r, j, 4:5], ALU.mult
                                  ).then_inc(rs_done, 1)

            def finish(b, c, j):
                t = b * NT + c * TC + j
                r = nrows(c, j)
                dve.wait_ge(rs_done, t + 1)
                dve.wait_ge(zb_ready, t + 1)
                T = c * TC + j
                dve.wait_ge(x2_done, 2 + t - (T > 0))
                dve.wait_ge(o_ready, t + 1)
                dve.scalar_tensor_tensor(out=zs[0:r, T % 2, :], in0=ps[0:r, OB, 0:D], scalar=smax[0:r, j, 5:6],
                                         in1=z_at(t, r), op0=ALU.mult, op1=ALU.add).then_inc(o_done, 1)
                dve.wait_ge(o_done, t + 1)
                dve.bn_stats(st2[0:r, j, :], zs[0:r, T % 2, :]).then_inc(st2_done, 1)
                dve.tensor_copy(z_at(t, r), zs[0:r, T % 2, :]).then_inc(z_back, 1)
                wait_apart(dve, st2_done, t + 1)
                dve.bn_aggr(mv2[0:r, j, :], st2[0:r, j, :]).then_inc(mv2_done, 1)

            for c in range(NC):
                if c == 1:
                    dve.wait_ge(h_ready, NIT)
                add_tokens(0, c, [embed_psum(c * TC + j) for j in range(TC)])
                if c == 0:
                    moments(0, 0)
            normal1(0, 0)
            moments(0, 1)
            for c in range(NC):
                for j, bank in enumerate(TB):
                    low_xt(0, c, j, bank)
                copy_xT(0, c)
                if c < NC - 1:
                    normal1(0, c + 1)
                if c == 0:
                    moments(0, 2)
                value_sum(0, c, 0, SB[0])
                value_sum(0, c, 1, SB[1])
                low_v(0, c, 0)
                value_sum(0, c, 2, SB[2])
                low_v(0, c, 1)
                low_v(0, c, 2)
            low_g(0, 0)
            shift(0, 0, 0)

            def body(b, c, has_next):
                t = b * NT + c * TC
                more = has_next or c < NC - 1
                for j in range(TC):
                    invert_sum(b, c, j)
                    for u in range(NC):
                        dve.wait_ge(t_hi, NC * (t + j) + u + 1)
                        s = slice(TC * u, TC * (u + 1))
                        dve.tensor_tensor(PT_lo[:, s, :].rearrange("p a b -> p (a b)"), ps[:, TB[u], 0:CW],
                                          PT_hi[:, s, :].rearrange("p a b -> p (a b)").bitcast(F32), ALU.subtract
                                          ).then_inc(t_lo, 1)
                    mask_sum(b, c, j)
                    if j == 0:
                        shift(b, c, 1)
                        if has_next:
                            add_tokens(b + 1, c, [ps[:, bank, 0:D] for bank in (AUX, T0, T1)])
                            moments(b + 1, c)
                    if j == 1:
                        if has_next:
                            normal1(b + 1, c)
                        finish(b, c, 0)
                        if has_next:
                            low_xt(b + 1, c, 0, AUX)
                        shift(b, c, 2)
                        if more:
                            low_g(*nxt(b, c))
                        if has_next:
                            low_xt(b + 1, c, 1, T0)
                            low_xt(b + 1, c, 2, T1)
                            copy_xT(b + 1, c)
                        finish(b, c, 1)
                        if has_next:
                            value_sum(b + 1, c, 0, AUX)
                            low_v(b + 1, c, 0)
                    if j == 2:
                        if more:
                            shift(*nxt(b, c), 0)
                        if has_next:
                            value_sum(b + 1, c, 1, T0)
                            value_sum(b + 1, c, 2, T1)
                            low_v(b + 1, c, 1)
                            low_v(b + 1, c, 2)
                        finish(b, c, 2)

            batches(dve, body)

            def low_w1(b):
                v = "p a b -> p (a b)"
                for k in range(TOPK):
                    dve.wait_ge(w1_hid, TOPK * b + k + 1)
                    dve.tensor_tensor(w1_lo[:, k].rearrange(v), w1_raw[:, k].rearrange(v),
                                      w1_hi[:, k].rearrange(v).bitcast(F32), ALU.subtract).then_inc(w1_lod, 1)

            def take_b1(b):
                dve.wait_ge(b1_in, 16 * TOPK * (b + 1))
                dve.tensor_copy(b1_cur[:], b1_sb[:, bass.ds(b * NF, NF)]).then_inc(cur_b1, 1)

            def take_w(b):
                dve.tensor_copy(w_cur[:], route_w[:, bass.ds(b * TOPK, TOPK)]).then_inc(cur_w, 1)

            def low_w2(b, k):
                wait_apart(dve, w2_hid, TOPK * b + k + 1)
                dve.scalar_tensor_tensor(out=w2_at(w2_lo, b, k), in0=w2_raw[:, k].rearrange("p a b -> p (a b)"),
                                         scalar=w_cur[:, k:k + 1], in1=w2_at(w2_hi, b, k).bitcast(F32),
                                         op0=ALU.mult, op1=ALU.subtract).then_inc(w2_lod, 1)

            def sum_b2(b):
                dve.wait_ge(b2_in, 16 * TOPK * (b + 1))
                dve.tensor_scalar(b2_sum[:], b2_raw[:, 0, :], route_w[:, bass.ds(b * TOPK, 1)], None, ALU.mult
                                  ).then_inc(b2_half, 1)
                dve.wait_ge(b2_half, b + 1)
                dve.scalar_tensor_tensor(out=b2_sum[:], in0=b2_raw[:, 1, :], scalar=route_w[:, bass.ds(b * TOPK + 1, 1)],
                                         in1=b2_sum[:], op0=ALU.mult, op1=ALU.add).then_inc(b2_done, 1)

            def low_xf(b, c, h):
                w = width(c)
                dve.wait_ge(xf_hid, DH * (b * NC + c) + h + 1)
                dve.tensor_tensor(xf_lo[:, h, 0:w], ps[:, XB, 0:w], xf_hi[:, h, 0:w].bitcast(F32), ALU.subtract
                                  ).then_inc(xf_lod, 1)

            def ln3(b, c, j):
                t = b * NT + c * TC + j
                r = nrows(c, j)
                dve.wait_ge(x2b_ready, t + 1)
                dve.wait_ge(out_ready, t + 1)
                dve.wait_ge(y_ready, t + 1)
                dve.tensor_tensor(yb[0:r, j, :], ps[0:r, Y0 + j, 0:D], x2b[0:r, j, :], ALU.add).then_inc(y_done, 1)
                dve.wait_ge(y_done, TC + t + 1)
                dve.bn_stats(st3[0:r, j, :], yb[0:r, j, :]).then_inc(st3_done, 1)
                wait_apart(dve, st3_done, t + 1)
                dve.bn_aggr(mv3[0:r, j, :], st3[0:r, j, :]).then_inc(mv3_done, 1)

            def norm3(b, c, j):
                t = b * NT + c * TC + j
                r = nrows(c, j)
                dve.wait_ge(rs3_done, t + 1)
                dve.tensor_scalar(yb[0:r, j, :], yb[0:r, j, :], mv3[0:r, j, 0:1], rs3[0:r, j:j + 1],
                                  ALU.subtract, ALU.mult).then_inc(nrm_done, 1)
                dve.wait_ge(nrm_done, t + 1)
                dve.tensor_tensor(yb[0:r, j, :], yb[0:r, j, :], gamma_row[0:r, :], ALU.mult).then_inc(gam_done, 1)

            def make_x2s(b, c, j):
                t = b * NT + c * TC + j
                r = nrows(c, j)
                dve.wait_ge(x2b_ready, b * NT + (c - 1) * TC + j + 1)
                dve.tensor_scalar(x2s[0:r, j, :], z_at(t, r), rstd2[0:r, bass.ds(t, 1)], nmr2[0:r, bass.ds(t, 1)],
                                  ALU.mult, ALU.add).then_inc(x2s_ready, 1)

            dve.wait_ge(kept2, 2 * TC)
            for j in range(TC):
                dve.tensor_scalar(x2s[:, j, :], z_at(j, P), rstd2[:, j:j + 1], nmr2[:, j:j + 1], ALU.mult, ALU.add
                                  ).then_inc(x2s_ready, 1)
            low_xf(0, 0, 0)
            low_xf(0, 0, 1)

            rstep = [0]

            def rlink(ins):
                rstep[0] += 1
                ins.then_inc(r_v, 1)
                dve.wait_ge(r_v, rstep[0])

            sm = lambda i: small[:, i, :]
            dve.wait_ge(r_pe, 1)
            rlink(dve.tensor_scalar(meanT[:], ps[:, 0, 0:DH * NB].rearrange("p (h b) -> p h b", h=DH), 1.0 / S, None,
                                    ALU.mult))
            dve.wait_ge(r_pe, 2)
            rlink(dve.tensor_tensor(sm(0), ps[0:NB, 1, 0:NE], br_row[:], ALU.add))
            rlink(dve.reduce_max(small[:, 9, 2:3], sm(0), AX_X))
            rlink(dve.tensor_scalar(small[:, 9, 0:1], small[:, 9, 2:3], -1.0, None, ALU.mult))
            dve.wait_ge(r_a, 1)
            rlink(dve.reciprocal(small[:, 9, 3:4], small[:, 9, 1:2]))
            rlink(dve.tensor_scalar(sm(2), sm(1), small[:, 9, 3:4], None, ALU.mult))
            dve.wait_ge(r_pe, 3)
            rlink(dve.tensor_scalar(sm(5), ps[0:NB, 2, 0:NE], float(S), None, ALU.mult))
            rlink(dve.reciprocal(sm(8), sm(5)))
            rlink(dve.tensor_scalar(sm(12), sm(8), CAPACITY, 1.0, ALU.mult, ALU.min))
            rlink(dve.tensor_tensor(sm(3), sm(2), sm(12), ALU.mult))
            rlink(dve.reduce_max(small[:, 10, 2:3], sm(3), AX_X))
            rlink(dve.tensor_scalar(small[:, 10, 0:1], small[:, 10, 2:3], -1.0, None, ALU.mult))
            dve.wait_ge(r_a, 2)
            rlink(dve.reciprocal(small[:, 10, 3:4], small[:, 10, 1:2]))
            rlink(dve.tensor_scalar(sm(13), sm(4), small[:, 10, 3:4], None, ALU.mult))
            rlink(dve.max(sm(6), sm(13)))
            rlink(dve.max_index(top_i[:], sm(6), sm(13)))
            rlink(dve.tensor_scalar(small[:, 11, 0:1], small[:, 6, 0:1], -1.0, None, ALU.mult))
            dve.wait_ge(r_a, 3)
            rlink(dve.reciprocal(small[:, 11, 3:4], small[:, 11, 1:2]))
            rlink(dve.tensor_scalar(small[:, 14, 0:TOPK], small[:, 7, 0:TOPK], small[:, 11, 3:4], None, ALU.mult))
            for k in range(TOPK):
                rlink(dve.tensor_scalar(diag_w[:, :, k], ident[0:NB, 0:NB], small[:, 14, k:k + 1], None, ALU.mult))
            dve.wait_ge(r_pe, 4)
            rlink(dve.tensor_copy(route_w[:], ps[:, 3, 0:NB * TOPK]))

            take_w(0)
            take_b1(0)
            low_w1(0)
            sum_b2(0)
            low_w2(0, 0)
            low_w2(0, 1)
            dve.wait_ge(ld_ffn, 32)
            dve.memset(st3[:, 0, :], 0.0).then_inc(h_lod, 4)
            dve.memset(st3[:, 1, :], 0.0).then_inc(y_done, TC)

            def ffn(b, c, has_next):
                n = NF * (b * NC + c)
                w = width(c)
                more = has_next or c < NC - 1
                for f in range(NF + 1):
                    if NHA <= f < NF:
                        dve.wait_ge(gelu_done, n + f + 1)
                        dve.tensor_copy(h_hi[:, f, 0:w], gel[:, f % 4, 0:w]).then_inc(h_hid, 1)
                    if f:
                        g = f - 1
                        if g < NHA:
                            dve.wait_ge(h_hid_act, NHA * (b * NC + c) + g + 1)
                        else:
                            dve.wait_ge(h_hid, (NF - NHA) * (b * NC + c) + g - NHA + 1)
                        dve.tensor_tensor(h_lo[:, g, 0:w], gel[:, g % 4, 0:w], h_hi[:, g, 0:w].bitcast(F32),
                                          ALU.subtract).then_inc(h_lod, 1)
                    if more and 1 <= f < 1 + TC:
                        make_x2s(*nxt(b, c), f - 1)
                if more:
                    low_xf(*nxt(b, c), 0)
                if c == 0 and has_next:
                    take_w(b + 1)
                if c == NC - 1 and has_next:
                    take_b1(b + 1)
                    low_w1(b + 1)
                    dve.wait_ge(x2b_ready, NT * (b + 1))
                    sum_b2(b + 1)
                ln3(b, c, 0)
                if more:
                    low_xf(*nxt(b, c), 1)
                if c == 1 and has_next:
                    low_w2(b + 1, 0)
                ln3(b, c, 1)
                norm3(b, c, 0)
                if c == 1 and has_next:
                    low_w2(b + 1, 1)
                ln3(b, c, 2)
                norm3(b, c, 1)
                norm3(b, c, 2)

            batches(dve, ffn)

        @block.tensor
        def _(pe):
            def turn(dst, src, rows):
                return pe.transpose(dst[:, 0:rows], src[0:rows], ident[0:rows, 0:rows])

            pe.wait_ge(c_ident, 1)
            for g in range(NPG):
                if g % GPI == 0:
                    pe.wait_ge(im_act if g else im_dve, 1)
                if g >= 4:
                    pe.wait_ge(pt_odd if g % 2 else pt_even, (g - 4) // 2 + 1)
                for k in range(4):
                    j = (g % GPI) * 4 + k
                    m = turn(ps[0:PD, g % 4, k * P:(k + 1) * P], imp[:, g // GPI, j, :], P)
                m.then_inc(pt_ready, 1)

            pe.wait_ge(ld_w, 16 * 12)
            for ho in range(DH):
                for he in range(DH):
                    m = pe.transpose(ps[:, 4, he * D + ho * P:he * D + (ho + 1) * P],
                                     wo_sb[:, ho, he * P:(he + 1) * P], ident[:])
            m.then_inc(su_pe, 1)
            for h in range(DH):
                m = pe.transpose(ps[0:PD, 5, h * P:(h + 1) * P], wt_sb[:, h, :], ident[:])
            m.then_inc(su_pe, 1)
            for hd in range(DH):
                for he in range(DH):
                    m = pe.matmul(ps[:, 6, hd * D:(hd + 1) * D], wq_sb[:, he, hd * P:(hd + 1) * P], wk_sb[:, he, :],
                                  start=(he == 0), stop=(he == DH - 1))
            m.then_inc(su_pe, 1)
            pe.wait_ge(su_wot, 1)
            for hd in range(DH):
                for he in range(DH):
                    m = pe.matmul(ps[:, 7, hd * D:(hd + 1) * D], wv_sb[:, he, hd * P:(hd + 1) * P], woT[:, he, :],
                                  start=(he == 0), stop=(he == DH - 1))
            m.then_inc(su_pe, 1)
            pe.wait_ge(su_wtt, 1)
            for hd in range(DH):
                d = slice(hd * P, (hd + 1) * P)
                pe.matmul(ps[:, 5, hd * 4:hd * 4 + 1], wq_sb[:, 0, d], ident[:, 0:1], start=True, stop=True)
                pe.matmul(ps[:, 5, hd * 4 + 1:hd * 4 + 2], wk_sb[:, 0, d], ident[:, 0:1], start=True, stop=True)
                for he in range(DH):
                    pe.matmul(ps[:, 5, hd * 4 + 2:hd * 4 + 3], wq_sb[:, he, d], bcol[:, 1, he:he + 1],
                              start=(he == 0), stop=(he == DH - 1))
                for he in range(DH):
                    m = pe.matmul(ps[:, 5, 16 + hd:17 + hd], wk_sb[:, he, d], bcol[:, 0, he:he + 1],
                                  start=(he == 0), stop=(he == DH - 1))
            m.then_inc(su_pe, 1)
            pe.wait_ge(su_bbc, 4)
            for he in range(DH):
                pe.matmul(ps[:, 4, 0:D], bbc[:, 1, he, :], woT[:, he, :], start=(he == 0), stop=(he == DH - 1))
            for he in range(DH):
                m = pe.matmul(ps[:, 4, D:D + 1], bbc[:, 0, he, :], bcol[:, 1, he:he + 1],
                              start=(he == 0), stop=(he == DH - 1))
            m.then_inc(su_pe, 1)
            pe.wait_ge(su_done, 1)

            def three(dst, lhs, rhs):
                n = 0
                for h in range(DH):
                    for a, r in ((0, 0), (0, 1), (1, 0)):
                        m = pe.matmul(dst, lhs[a][h], rhs[r][h], start=(n == 0), stop=(n == 3 * DH - 1))
                        n += 1
                return m

            def embed(c, j, bank):
                m = pe.matmul(ps[:, bank, 0:D], pst[:, j * P:(j + 1) * P], wtT[:], start=True, stop=True)
                m.then_inc(h_ready, 1)

            def turn_xn(b, c, j, bank):
                r = nrows(c, j)
                pe.wait_ge(xn_ready, b * NT + c * TC + j + 1)
                for h in range(DH):
                    m = turn(ps[:, bank, h * P:(h + 1) * P], xn[:, j, h * P:(h + 1) * P], r)
                m.then_inc(xt_ready, 1)

            def values(b, c, j, bank):
                r = nrows(c, j)
                pe.wait_ge(xt_lo, b * NT + c * TC + j + 1)
                s = slice(j * P, j * P + r)
                three(ps[0:r, bank, 0:VW], [[X[:, h, s] for h in range(DH)] for X in (xs_hi, xs_lo)],
                      [[W[:, h, :] for h in range(DH)] for W in (WV_hi, WV_lo)]).then_inc(v_ready, 1)

            def queries(b, c, second=()):
                w = width(c) + width(c) % 2
                pe.wait_ge(xt_copied, 2 * (b * NC + c + 1))
                for hd, bank in ((0, T2), (1, AUX)):
                    if hd:
                        for s, v in second:
                            pe.wait_ge(s, v)
                    three(ps[:, bank, 0:w], [[A[:, h, hd * P:(hd + 1) * P] for h in range(DH)] for A in (A_hi, A_lo)],
                          [[xT_at(X, b, h, c * CW, w) for h in range(DH)] for X in (xT_hi, xT_lo)]).then_inc(g_ready, 1)

            def scores_of(b, c, j):
                r = nrows(c, j)
                pe.wait_ge(g_lo, DH * (b * NC + c + 1))
                if c == 0 and j == 0:
                    pe.wait_ge(xt_copied, 2 * NC * (b + 1))
                s = slice(j * P, j * P + r)
                for n in range(3):
                    m = three(ps[0:r, n, 0:SW + 1], [[G[:, h, s] for h in range(DH)] for G in (G_hi, G_lo)],
                              [[xT_at(X, b, h, n * SW, SW + 1) for h in range(DH)] for X in (xT_hi, xT_lo)])
                m.then_inc(s_ready, 1)

            def turn_probs(b, c, j, before):
                t = b * NT + c * TC + j
                r = nrows(c, j)
                pe.wait_ge(exp_done, t + 1)
                for u in range(NC):
                    for s, v in before[u]:
                        pe.wait_ge(s, v)
                    for k in range(TC):
                        kt = u * TC + k
                        m = turn(ps[:, TB[u], k * P:(k + 1) * P], probs[:, kt * P:(kt + 1) * P], r)
                    m.then_inc(t_ready, 1)

            def attend(b, c, j):
                t = b * NT + c * TC + j
                r = nrows(c, j)
                if c == 0 and j == 0:
                    pe.wait_ge(v_lo, NT * (b + 1))
                if j == 1:
                    pe.wait_ge(o_done, t)
                n = 0
                for u in range(NC):
                    pe.wait_ge(t_lo, NC * t + u + 1)
                    for kt in range(u * TC, (u + 1) * TC):
                        kr = LASTR if kt == NT - 1 else P
                        for PT, V in ((PT_hi, V_hi), (PT_hi, V_lo), (PT_lo, V_hi)):
                            m = pe.matmul(ps[0:r, OB, 0:D], PT[0:kr, kt, 0:r], v_at(V, b, kt, kr),
                                          start=(n == 0), stop=(n == 3 * NT - 1))
                            n += 1
                m.then_inc(o_ready, 1)

            def turn_x2(b, c, h):
                m = b * NC + c
                pe.wait_ge(x2s_ready, TC * (m + 1))
                for j in range(TC):
                    r = nrows(c, j)
                    i = turn(ps[:, XB, j * P:(j + 1) * P], x2s[:, j, h * P:(h + 1) * P], r)
                i.then_inc(xf_ready, 1)

            def sum_tokens(b):
                for h in range(DH):
                    m = pe.matmul(ps[:, 0, h * NB + b:h * NB + b + 1], acc[:, b, h * P:(h + 1) * P], ones[:, 0:1],
                                  start=True, stop=True)
                return m

            pe.wait_ge(pt_even, NPG // 2)
            pe.wait_ge(pt_odd, NPG // 2)
            for T in range(NIT):
                pe.matmul(embed_psum(T), patches(0, T * P, P), wtT[:], start=True, stop=True).then_inc(h_ready, 1)
            pe.wait_ge(h_done, NIT)
            for c in range(NC):
                for j, bank in enumerate(TB):
                    turn_xn(0, c, j, bank)
                if c:
                    pe.wait_ge(v_f, c * TC)
                for j, bank in enumerate(SB):
                    values(0, c, j, bank)
            pe.wait_ge(v_f, NT)
            queries(0, 0)
            scores_of(0, 0, 0)

            def body(b, c, has_next):
                t = b * NT + c * TC
                more = has_next or c < NC - 1
                pn = (b + 1) * NT + c * TC if has_next else NB * NT
                hn = (b + 1) * NIT + c * TC
                m = b * NC + c
                bn, cn = nxt(b, c)

                turn_probs(b, c, 0, [[(v_f, pn - 1)], [(v_f, pn)], []])
                scores_of(b, c, 1)
                if has_next:
                    pe.wait_ge(pst_ready, b * NC + c + 1)
                    embed(c, 0, AUX)
                    pe.wait_ge(t_lo, NC * t + 1)
                    embed(c, 1, T0)
                    if c < NC - 1:
                        pe.wait_ge(t_lo, NC * t + 2)
                        embed(c, 2, T1)
                attend(b, c, 0)

                nh = min(TC, NIT - c * TC)
                turn_probs(b, c, 1, [[(h_done, hn + 2)], [(h_done, hn + nh)], []] if has_next else [[], [], []])
                scores_of(b, c, 2)
                if has_next:
                    pe.wait_ge(h_done, hn + 1)
                    turn_xn(b + 1, c, 0, AUX)
                    pe.wait_ge(t_lo, NC * (t + 1) + 1)
                    turn_xn(b + 1, c, 1, T0)
                    pe.wait_ge(t_lo, NC * (t + 1) + 2)
                    turn_xn(b + 1, c, 2, T1)
                if more:
                    pe.wait_ge(t_lo, NC * (t + 1) + 3)
                    queries(bn, cn, [(xt_lo, pn + 1)] if has_next else [])
                attend(b, c, 1)
                if has_next:
                    pe.wait_ge(g_lo, DH * (m + 2))
                    values(b + 1, c, 0, AUX)

                turn_probs(b, c, 2, [[(xt_lo, pn + 2)], [(xt_lo, pn + 3)], [(g_lo, DH * (m + 1) + 1)]]
                           if has_next else [[], [], [(g_lo, DH * (m + 1) + 1)] if more else []])
                if more:
                    scores_of(bn, cn, 0)
                if has_next:
                    pe.wait_ge(t_lo, NC * (t + 2) + 1)
                    values(b + 1, c, 1, T0)
                    pe.wait_ge(t_lo, NC * (t + 2) + 2)
                    values(b + 1, c, 2, T1)
                elif c == NC - 1:
                    pe.wait_ge(acc_done, (NB - 1) * NT)
                    for e in range(NB - 1):
                        sum_tokens(e)
                attend(b, c, 2)

            batches(pe, body)

            turn_x2(0, 0, 0)
            pe.wait_ge(xf_lod, 1)
            turn_x2(0, 0, 1)
            pe.wait_ge(acc_done, NB * NT)
            sum_tokens(NB - 1).then_inc(r_pe, 1)
            pe.wait_ge(r_v, 1)
            for h in range(DH):
                m = pe.matmul(ps[0:NB, 1, 0:NE], meanT[:, h, :], wr_sb[:, h, :], start=(h == 0), stop=(h == DH - 1))
            m.then_inc(r_pe, 1)
            pe.wait_ge(r_v, 6)
            pe.matmul(ps[0:NB, 2, 0:NE], ones[0:NB, 0:NB], small[:, 2, :], start=True, stop=True).then_inc(r_pe, 1)
            pe.wait_ge(r_v, 21)
            pe.matmul(ps[:, 3, 0:NB * TOPK], ones[0:NB, :], diag_w[:].rearrange("p b k -> p (b k)"),
                      start=True, stop=True).then_inc(r_pe, 1)

            def ffn(b, c, has_next):
                m = b * NC + c
                n = NF * m
                t = b * NT + c * TC
                w = width(c) + width(c) % 2
                more = has_next or c < NC - 1
                pe.wait_ge(xf_lod, DH * (m + 1))
                for f in range(NF):
                    k, q = f // FQ, f % FQ
                    if c == 0 and q == 0:
                        pe.wait_ge(w1_lod, TOPK * b + k + 1)
                    if f >= 4:
                        pe.wait_ge(gelu_done, n + f - 3)
                    three(ps[:, f % 4, 0:w],
                          [[W[:, k, h, q * P:(q + 1) * P] for h in range(DH)] for W in (w1_hi, w1_lo)],
                          [[X[:, h, 0:w] for h in range(DH)] for X in (xf_hi, xf_lo)]).then_inc(f_ready, 1)
                if more:
                    turn_x2(*nxt(b, c), 0)
                for j in range(TC):
                    r = nrows(c, j)
                    pe.wait_ge(y_done, t + j + 1)
                    i = 0
                    for f in range(NF):
                        if j == 0:
                            pe.wait_ge(h_lod, 4 + n + f + 1)
                            if c == 0 and f % FQ == 0:
                                pe.wait_ge(w2_lod, TOPK * b + f // FQ + 1)
                        k, q = f // FQ, f % FQ
                        for H, W in ((h_hi, w2_hi), (h_hi, w2_lo), (h_lo, w2_hi)):
                            ins = pe.matmul(ps[0:r, Y0 + j, 0:D], H[:, f, j * P:j * P + r],
                                            w2_at(W, b, k)[:, q * D:(q + 1) * D],
                                            start=(i == 0), stop=(i == 3 * NF - 1))
                            i += 1
                    ins.then_inc(y_ready, 1)
                    if j == 0 and more:
                        pe.wait_ge(xf_lod, DH * (m + 1) + 1)
                        turn_x2(*nxt(b, c), 1)

            batches(pe, ffn)


_INS = ["x", "txt"] + ["L0_tok_W", "L0_tok_b", "L0_tok_pos"] + \
    ["L0_attn_" + n for n in ("Wq", "bq", "Wk", "bk", "Wv", "bv", "Wo", "bo")] + \
    ["L0_ffn_" + n for n in ("Wr", "br", "W1", "b1", "W2", "b2", "gamma", "beta")]


def kernel(**inputs):
    import numpy as np
    import concourse.bacc as bacc
    from concourse import mybir as mb
    from concourse.bass_utils import run_bass_kernel_spmd as run

    nc = bacc.Bacc("TRN2", target_bir_lowering=False, num_devices=1)
    arrays, args = {}, []
    for name in _INS:
        a = np.ascontiguousarray(inputs[name])
        arrays[f"in_{name}"] = a
        args.append(nc.dram_tensor(f"in_{name}", a.shape, mb.dt.from_np(a.dtype), kind="ExternalInput").ap())
    args.append(nc.dram_tensor("out_0", (NB, S, D), F32, kind="ExternalOutput").ap())
    build(nc, *args)
    return run(nc, [arrays], core_ids=[0]).results[0]["out_0"]
```
